# Optimizing a Trainium2 kernel written in Bass

```python
import numpy as np
import jax
import jax.numpy as jnp

def _softmax(x, axis=-1):
    return jax.nn.softmax(x, axis=axis)

def _gelu(x):
    return jax.nn.gelu(x, approximate=True)

def _silu(x):
    return jax.nn.silu(x)

def _sigmoid(x):
    return jax.nn.sigmoid(x)

def _layernorm(x, axis=-1, eps=1e-05):
    m = jnp.mean(x, axis=axis, keepdims=True)
    v = jnp.var(x, axis=axis, keepdims=True)
    return (x - m) / jnp.sqrt(v + eps)

def _scatter_add(tgt, idx, src, axis=0):
    return tgt.at[idx].add(src)

def _segment_sum(src, seg, n):
    return jax.ops.segment_sum(src, seg, n)
kernel_name = 'mk_vit_tower_d1_tok_img768_r4_055f72'

def setup_inputs(seed: int=0):
    np.random.seed(seed)
    _w = jnp.asarray

    def _rec_inputs():
        import jax
        import jax.numpy as jnp
        _rk = jax.random.key(seed)
        x = -0.000147625 + 0.999875 * jax.random.normal(jax.random.fold_in(_rk, 1), (64, 12, 224, 224), jnp.float32)
        return x
    x = _rec_inputs()

    def _L0_tok_setup():
        import jax, jax.numpy as jnp
        import numpy as np
        IMG = 224
        PATCH = 16
        EMBED = 192
        C = 12
        B = 64
        key = jax.random.key(seed)
        k1, k2 = jax.random.split(key)
        x = jax.random.normal(k1, (B, C, IMG, IMG), dtype=jnp.float32)
        channel_weights = jax.random.normal(k2, (C, EMBED), dtype=jnp.float32)
        return {'x': x, 'channel_weights': channel_weights}
    _L0_tok_all = _L0_tok_setup()
    _L0_tok_in = {k: v for k, v in _L0_tok_all.items() if k in ('channel_weights',)}
    del _L0_tok_all

    def _L0_attn_setup():
        import math
        import jax, jax.numpy as jnp
        import numpy as np
        B, N, D_IN, D_OUT = (8, 512, 192, 192)
        key = jax.random.key(seed)
        k1, k2, k3 = jax.random.split(key, 3)
        x = jax.random.normal(k1, (B, N, D_IN), dtype=jnp.float32)
        W_qkv = jax.random.normal(k2, (D_IN, 3 * D_OUT), dtype=jnp.float32) * (1.0 / math.sqrt(D_IN))
        b_qkv = jax.random.normal(k3, (3 * D_OUT,), dtype=jnp.float32) * 0.02
        return {'x': x, 'W_qkv': W_qkv, 'b_qkv': b_qkv}
    _L0_attn_all = _L0_attn_setup()
    _L0_attn_in = {k: v for k, v in _L0_attn_all.items() if k in ('W_qkv', 'b_qkv')}
    del _L0_attn_all

    def _L0_ffn_setup():
        import math
        import jax, jax.numpy as jnp
        import numpy as np
        EMBED_CHOICES = [96, 144, 192]
        RATIO_CHOICES = [2, 3, 4]
        E_MAX = 192
        H_MAX = 768

        def new_gelu(x):
            c = math.sqrt(2.0 / math.pi)
            return 0.5 * x * (1.0 + jnp.tanh(c * (x + 0.044715 * x * x * x)))

        def _mixed_coeffs(alpha_e, alpha_r):
            h_idx = jnp.arange(H_MAX)
            d_idx = jnp.arange(E_MAX)
            C0 = jnp.zeros((H_MAX, E_MAX), jnp.float32)
            c0b = jnp.zeros((H_MAX,), jnp.float32)
            C1 = jnp.zeros((E_MAX, H_MAX), jnp.float32)
            c1b = jnp.zeros((E_MAX,), jnp.float32)
            for i, e in enumerate(EMBED_CHOICES):
                m_in = (d_idx < e).astype(jnp.float32)
                for j, r in enumerate(RATIO_CHOICES):
                    a = alpha_e[i] * alpha_r[j]
                    m_out = (h_idx < r * e).astype(jnp.float32)
                    C0 = C0 + a * (m_out[:, None] * m_in[None, :])
                    c0b = c0b + a * m_out
                    C1 = C1 + a * (m_in[:, None] * m_out[None, :])
                    c1b = c1b + a * m_in
            return (C0, c0b, C1, c1b)
        key = jax.random.key(seed)
        ks = jax.random.split(key, 6)
        x = jax.random.normal(ks[0], (8, 512, E_MAX), jnp.float32)
        w_fc = jax.random.normal(ks[1], (H_MAX, E_MAX), jnp.float32) * 0.02
        b_fc = jnp.zeros((H_MAX,), jnp.float32)
        w_proj = jax.random.normal(ks[2], (E_MAX, H_MAX), jnp.float32) * 0.02
        b_proj = jnp.zeros((E_MAX,), jnp.float32)
        alpha_e = jax.nn.softmax(jax.random.normal(ks[3], (3,), jnp.float32))
        alpha_r = jax.nn.softmax(jax.random.normal(ks[4], (3,), jnp.float32))
        return {'x': x, 'w_fc': w_fc, 'b_fc': b_fc, 'w_proj': w_proj, 'b_proj': b_proj, 'alpha_e': alpha_e, 'alpha_r': alpha_r}
    _L0_ffn_all = _L0_ffn_setup()
    _L0_ffn_in = {k: v for k, v in _L0_ffn_all.items() if k in ('w_fc', 'b_fc', 'w_proj', 'b_proj', 'alpha_e', 'alpha_r')}
    del _L0_ffn_all
    return {'x': x, 'L0_tok_channel_weights': _L0_tok_in['channel_weights'], 'L0_attn_W_qkv': _L0_attn_in['W_qkv'], 'L0_attn_b_qkv': _L0_attn_in['b_qkv'], 'L0_ffn_w_fc': _L0_ffn_in['w_fc'], 'L0_ffn_b_fc': _L0_ffn_in['b_fc'], 'L0_ffn_w_proj': _L0_ffn_in['w_proj'], 'L0_ffn_b_proj': _L0_ffn_in['b_proj'], 'L0_ffn_alpha_e': _L0_ffn_in['alpha_e'], 'L0_ffn_alpha_r': _L0_ffn_in['alpha_r']}

def reference(x, L0_tok_channel_weights, L0_attn_W_qkv, L0_attn_b_qkv, L0_ffn_w_fc, L0_ffn_b_fc, L0_ffn_w_proj, L0_ffn_b_proj, L0_ffn_alpha_e, L0_ffn_alpha_r):
    import jax
    import jax.numpy as jnp

    def _L0_tok_ref(x, channel_weights):
        import jax, jax.numpy as jnp
        import numpy as np
        IMG = 224
        PATCH = 16
        EMBED = 192
        C = 12
        B = 64
        Bb, Cc, H, W = x.shape
        K = PATCH
        n = H // K
        pooled = x.reshape(Bb, Cc, n, K, n, K).sum(axis=(3, 5))
        out = jnp.einsum('bcij,ce->bije', pooled, channel_weights)
        return out.reshape(Bb, n * n, EMBED)

    def _L0_attn_ref(x, W_qkv, b_qkv):
        import math
        import jax, jax.numpy as jnp
        import numpy as np
        B, N, D_IN, D_OUT = (8, 512, 192, 192)
        d_out = D_OUT
        qkv = jnp.einsum('bnd,de->bne', x, W_qkv) + b_qkv
        q = qkv[:, :, :d_out]
        k = qkv[:, :, d_out:2 * d_out]
        v = qkv[:, :, 2 * d_out:3 * d_out]
        scale = 1.0 / math.sqrt(d_out)
        scores = jnp.einsum('bqd,bkd->bqk', q, k) * scale
        attn = jax.nn.softmax(scores, axis=-1)
        context = jnp.einsum('bqk,bkd->bqd', attn, v)
        return context

    def _L0_ffn_ref(x, w_fc, b_fc, w_proj, b_proj, alpha_e, alpha_r):
        import math
        import jax, jax.numpy as jnp
        import numpy as np
        EMBED_CHOICES = [96, 144, 192]
        RATIO_CHOICES = [2, 3, 4]
        E_MAX = 192
        H_MAX = 768

        def new_gelu(x):
            c = math.sqrt(2.0 / math.pi)
            return 0.5 * x * (1.0 + jnp.tanh(c * (x + 0.044715 * x * x * x)))

        def _mixed_coeffs(alpha_e, alpha_r):
            h_idx = jnp.arange(H_MAX)
            d_idx = jnp.arange(E_MAX)
            C0 = jnp.zeros((H_MAX, E_MAX), jnp.float32)
            c0b = jnp.zeros((H_MAX,), jnp.float32)
            C1 = jnp.zeros((E_MAX, H_MAX), jnp.float32)
            c1b = jnp.zeros((E_MAX,), jnp.float32)
            for i, e in enumerate(EMBED_CHOICES):
                m_in = (d_idx < e).astype(jnp.float32)
                for j, r in enumerate(RATIO_CHOICES):
                    a = alpha_e[i] * alpha_r[j]
                    m_out = (h_idx < r * e).astype(jnp.float32)
                    C0 = C0 + a * (m_out[:, None] * m_in[None, :])
                    c0b = c0b + a * m_out
                    C1 = C1 + a * (m_in[:, None] * m_out[None, :])
                    c1b = c1b + a * m_in
            return (C0, c0b, C1, c1b)
        C0, c0b, C1, c1b = _mixed_coeffs(alpha_e, alpha_r)
        W0 = w_fc * C0
        b0 = b_fc * c0b
        h = jnp.einsum('bte,he->bth', x, W0) + b0
        h = new_gelu(h)
        W1 = w_proj * C1
        b1 = b_proj * c1b
        out = jnp.einsum('bth,eh->bte', h, W1) + b1
        return out
    h = _L0_tok_ref(x, L0_tok_channel_weights)
    h = h + _L0_attn_ref(_layernorm(h, axis=-1), L0_attn_W_qkv, L0_attn_b_qkv)
    h = h + _L0_ffn_ref(_layernorm(h, axis=-1), L0_ffn_w_fc, L0_ffn_b_fc, L0_ffn_w_proj, L0_ffn_b_proj, L0_ffn_alpha_e, L0_ffn_alpha_r)
    return h

_drawn_inputs = setup_inputs


def setup_inputs(seed=0):
    import zlib

    import numpy as np

    out = dict(_drawn_inputs(seed))
    spreads = {'L0_ffn_b_fc': (0.0, 0.8), 'L0_ffn_b_proj': (0.0, 2.0)}
    factors = {'L0_attn_W_qkv': 8.0,
     'L0_attn_b_qkv': 31.481,
     'L0_ffn_w_fc': 8.0,
     'L0_ffn_w_proj': 8.0,
     'L0_ffn_alpha_e': 8.0,
     'L0_ffn_alpha_r': 8.0}
    for name, (base, spread) in spreads.items():
        noise = np.random.default_rng([zlib.crc32(name.encode()), seed]).standard_normal(out[name].shape)
        drawn = base * np.exp(spread * noise) if base else spread * noise
        out[name] = jnp.asarray(drawn.astype(out[name].dtype))
    for name, factor in factors.items():
        out[name] = (out[name] * factor).astype(out[name].dtype)
    return out
```

```python
from contextlib import ExitStack

import numpy as np

import concourse.bass as bass
from concourse import mybir

F32 = mybir.dt.float32
F32R = mybir.dt.float32r
I32 = mybir.dt.int32
ALU = mybir.AluOpType
ACT = mybir.ActivationFunctionType
AX = mybir.AxisListType

IMAGES, CHANNELS, SIDE = 64, 12, 224
PATCH = 16
GRID = SIDE // PATCH
TOKENS = GRID * GRID
EMBED = 192
HIDDEN = 768
EPS = 1e-5
EMBED_CHOICES = (96, 144, 192)
RATIO_CHOICES = (2, 3, 4)
MIXES = len(EMBED_CHOICES) * len(RATIO_CHOICES)

GROUP = 4
GROUPS = IMAGES // GROUP
Q = 32
HALF = TOKENS // 2
PAIRS = 8
TILES = GROUP * CHANNELS // PAIRS
E2 = EMBED // 2
HT = HIDDEN // 128
PAIR_TOKENS = 2 * TOKENS

ONE_P = CHANNELS
CTX = CHANNELS
ONE_U = 2 * CHANNELS
BASIS = ONE_U + 1
ONE_F = BASIS

SEL_AT, MASK_G, MASK_S, LO_ACT, LO_W = 128, 896, 1024, 1152, 1153
FULL = 1154
ROW_P, ROW_C, ROW_ONE_U, ROW_ONE_P, ROW_ONE_F, ROW_IN = 0, 128, 256, 384, 512, 640
ROW_OUT = ROW_IN + EMBED
ROWS = ROW_OUT + HIDDEN

SLOTS = 12
MAGIC = float(0x5F3759DF)


def constants():
    full = np.zeros((128, FULL), np.float32)
    full[:, :128] = np.eye(128)
    for t in range(TILES):
        for p in range(128):
            b, c = divmod(PAIRS * t + p % PAIRS, CHANNELS)
            full[p, SEL_AT + 128 * t + Q * b + c] = 1.0
    block = np.kron(np.eye(GROUP), np.ones((Q, Q)))
    full[:, MASK_G:MASK_G + 128] = block / EMBED
    full[:, MASK_S:MASK_S + 128] = block / np.sqrt(EMBED)
    quadrant = np.arange(128) // Q
    full[:, LO_ACT] = -(quadrant % 2)
    full[:, LO_W] = -(quadrant // 2)
    rows = np.zeros((CHANNELS, ROWS), np.float32)
    for b in range(GROUP):
        for c in range(CHANNELS):
            rows[c, ROW_P + Q * b + c] = 1.0
            rows[c, ROW_C + Q * b + CTX + c] = 1.0
        rows[0, ROW_ONE_U + Q * b + ONE_U] = 1.0
        rows[0, ROW_ONE_P + Q * b + ONE_P] = 1.0
        rows[0, ROW_ONE_F + Q * b + ONE_F] = 1.0
    for i, e in enumerate(EMBED_CHOICES):
        for j, r in enumerate(RATIO_CHOICES):
            k = len(RATIO_CHOICES) * i + j
            rows[k, ROW_IN:ROW_IN + e] = 1.0
            rows[k, ROW_OUT:ROW_OUT + r * e] = 1.0
    return full, rows


def build(nc, x, cw, wqkv, bqkv, wfc, bfc, wproj, bproj, alpha_e, alpha_r, const_full, const_rows, out):
    with ExitStack() as ctx:
        def sb(name, shape, dt=F32):
            return ctx.enter_context(nc.sbuf_tensor(name, shape, dt))

        def sem(name):
            return ctx.enter_context(nc.semaphore(name))

        cf = sb("cf", [128, FULL])
        cr = sb("cr", [CHANNELS, ROWS])
        cw_sb = sb("cw_sb", [CHANNELS, EMBED])
        cw_mean = sb("cw_mean", [CHANNELS, 1])
        cwc = sb("cwc", [CHANNELS, EMBED])
        wqkv_sb = sb("wqkv_sb", [E2, 2, 3 * EMBED])
        bqkv_sb = sb("bqkv_sb", [1, 3 * EMBED])
        bfc_sb = sb("bfc_sb", [1, HIDDEN])
        wproj_sb = sb("wproj_sb", [E2, 2, HIDDEN])
        bproj_sb = sb("bproj_sb", [1, EMBED])
        alpha_sb = sb("alpha_sb", [MIXES, 2])
        mix = sb("mix", [MIXES, 1])
        mix_in = sb("mix_in", [MIXES, EMBED])
        cwt = sb("cwt", [E2, 2, 128])
        cwt_ctx = sb("cwt_ctx", [E2, 2, 128])
        qkt = sb("qkt", [E2, 4, 128])
        basis_mean = sb("basis_mean", [128, 1])
        basis_t = sb("basis_t", [E2, 2, 128])
        id_g1 = sb("id_g1", [128, 256])
        score_mat = sb("score_mat", [128, 128])
        g2 = sb("g2", [128, 128])
        resid = sb("resid", [128, EMBED])
        f_stack = sb("f_stack", [128, HIDDEN], F32R)
        w1_f32 = sb("w1_f32", [128, HT, EMBED])
        w1_hi = sb("w1_hi", [128, HT, EMBED], F32R)
        w1_lo = sb("w1_lo", [128, HT, EMBED], F32R)
        xs = sb("xs", [128, TILES, GRID, SIDE])
        pooled = sb("pooled", [128, TILES, TOKENS])
        p_rows = sb("p_rows", [128, TOKENS])
        u_tok = sb("u_tok", [HALF, 2, GROUP, Q])
        phat_tok = sb("phat_tok", [HALF, 2, GROUP, Q])
        uhat_tok = sb("uhat_tok", [HALF, 2, GROUP, 4, Q])
        prod = sb("prod", [HALF, 2, GROUP, Q])
        stat = sb("stat", [HALF, 4, 2 * GROUP])
        newton = sb("newton", [HALF, 2 * GROUP])
        phat_rows = sb("phat_rows", [128, TOKENS])
        b_rows = sb("b_rows", [128, TOKENS])
        neg_max = sb("neg_max", [HALF, GROUP, 2])
        probs = sb("probs", [HALF, GROUP, 2, TOKENS])
        probs_t = sb("probs_t", [HALF, GROUP, 2, TOKENS])
        three_halves = sb("three_halves", [HALF, 2 * GROUP])
        zero = sb("zero", [128, 1])
        row_inv = sb("row_inv", [HALF, 2, GROUP])
        u_rows = sb("u_rows", [128, TOKENS])
        u_kept = sb("u_kept", [128, TOKENS])
        uhat_hi = sb("uhat_hi", [128, GROUP * TOKENS], F32R)
        uhat_stack = sb("uhat_stack", [128, GROUP * TOKENS], F32R)
        h_f32 = sb("h_f32", [128, 2, PAIR_TOKENS])
        h_hi = sb("h_hi", [128, 2, HT, PAIR_TOKENS], F32R)
        h_lo = sb("h_lo", [128, 2, HT, PAIR_TOKENS], F32R)
        out_sb = sb("out_sb", [128, 2, GROUP, EMBED])
        w0t = probs[0:E2].rearrange("p b h k -> p (b h k)")[:, 0:2 * HIDDEN].rearrange("p (k h) -> p k h", k=2)
        coef = probs_t[0:E2].rearrange("p b k q -> p (b k q)")[:, 0:2 * HIDDEN].rearrange("p (k h) -> p k h", k=2)
        wfc_sb = out_sb[:].rearrange("p h b e -> p (h b) e")[:, 0:HT, :]
        basis_sb, basis_c = phat_rows[:, 0:EMBED], b_rows[:, 0:EMBED]
        f_hi = uhat_hi[:, 0:HIDDEN]

        ps = ctx.enter_context(nc.psum_tensor("ps", [128, 8, 512], F32))
        HB, OB = 4, 6

        x_landed = [sem(f"x_landed{t}") for t in range(TILES)]
        cf_landed = sem("cf_landed")
        cr_landed = sem("cr_landed")
        cw_landed = sem("cw_landed")
        wqkv_landed = sem("wqkv_landed")
        mix_landed = sem("mix_landed")
        wfc_landed = sem("wfc_landed")
        wproj_landed = sem("wproj_landed")
        setup_pe = sem("setup_pe")
        setup_act = sem("setup_act")
        setup_dve = sem("setup_dve")
        setup_pool = sem("setup_pool")
        setup_pool_self = sem("setup_pool_self")
        reduced = sem("reduced")
        pool_summed = sem("pool_summed")
        p_rows_ready = sem("p_rows_ready")
        tok_summed = sem("tok_summed")
        p_tok_ready = sem("p_tok_ready")
        stat_steps = sem("stat_steps")
        newton_steps = sem("newton_steps")
        phat_tok_ready = sem("phat_tok_ready")
        phat_turned = sem("phat_turned")
        phat_rows_ready = sem("phat_rows_ready")
        b_summed = sem("b_summed")
        b_rows_ready = sem("b_rows_ready")
        scores_ready = sem("scores_ready")
        max_ready = sem("max_ready")
        probs_ready = sem("probs_ready")
        probs_turned = sem("probs_turned")
        probs_t_ready = sem("probs_t_ready")
        context_ready = sem("context_ready")
        row_inv_ready = sem("row_inv_ready")
        u_tok_ready = sem("u_tok_ready")
        u_turned = sem("u_turned")
        u_rows_ready = sem("u_rows_ready")
        g2_summed = sem("g2_summed")
        uhat_tok_ready = sem("uhat_tok_ready")
        uhat_turned = sem("uhat_turned")
        uhat_hi_ready = sem("uhat_hi_ready")
        uhat_ready = sem("uhat_ready")
        u_kept_ready = sem("u_kept_ready")
        hidden_summed = sem("hidden_summed")
        gelu_done = sem("gelu_done")
        h_lo_ready = sem("h_lo_ready")
        out_summed = sem("out_summed")
        out_ready = sem("out_ready")
        out_sent = [sem("out_sent0"), sem("out_sent1")]

        ident = cf[:, 0:128]
        x_tiles = x.rearrange("(n b) c (i k) w -> n k (b c) i w", b=GROUP, k=PATCH)
        out_tiles = out.rearrange("(n b) (h p) e -> n p b h e", b=2, h=2)

        PE_CWT, PE_QKT, PE_COEF, PE_W0T, PE_G1, PE_A, PE_BASIS, PE_BT, PE_G2, PE_F, PE_W1 = range(1, 12)
        ACT_CWT, ACT_QKT, ACT_COEF, ACT_ROWS, ACT_W0T, ACT_BT, ACT_FHI, ACT_W1 = range(1, 9)

        block = ctx.enter_context(nc.Block())

        def first(n):
            return isinstance(n, int) and n == 0

        @block.sync
        def _(sp):
            def load(n, t):
                sp.dma_start(xs[:, t], x_tiles[n, :, PAIRS * t:PAIRS * (t + 1)]).then_inc(x_landed[t], 16)

            def reload(n, t):
                sp.wait_ge(reduced, SLOTS * (n - 1) + 2 * t + 2)
                load(n, t)

            def send(m, half):
                sp.wait_ge(out_ready, 8 * m + 4 * half + 4)
                sp.dma_start(out_tiles[2 * m + half],
                             out_sb[0:HALF, half].rearrange("p (b h) e -> p b h e", b=2)).then_inc(out_sent[half], 16)

            def iteration(n, loads=True, ffn=True, tail=True):
                for t in range(3):
                    if loads:
                        reload(n + 1, t)
                if tail:
                    send(n - 3, 1)
                for t in range(3, TILES):
                    if loads:
                        reload(n + 1, t)
                if ffn:
                    send(n - 2, 0)

            load(0, 0)
            sp.dma_start(cr[:], const_rows).then_inc(cr_landed, 16)
            sp.dma_start(cw_sb[:], cw).then_inc(cw_landed, 16)
            sp.dma_start(cf[:], const_full).then_inc(cf_landed, 16)
            sp.dma_start(alpha_sb[:, 0:1], alpha_e).then_inc(mix_landed, 16)
            sp.dma_start(alpha_sb[:, 1:2], alpha_r).then_inc(mix_landed, 16)
            sp.dma_start(bqkv_sb[:], bqkv).then_inc(wqkv_landed, 16)
            sp.dma_start(wqkv_sb[:], wqkv.rearrange("(k p) n -> p k n", k=2)).then_inc(wqkv_landed, 16)
            load(0, 1)
            sp.dma_start(bfc_sb[:], bfc).then_inc(wfc_landed, 16)
            sp.dma_start(wfc_sb, wfc.rearrange("(t p) e -> p t e", p=128)).then_inc(wfc_landed, 16)
            load(0, 2)
            sp.dma_start(bproj_sb[:], bproj).then_inc(wproj_landed, 16)
            sp.dma_start(wproj_sb[:], wproj.rearrange("(k p) h -> p k h", k=2)).then_inc(wproj_landed, 16)
            for t in range(3, TILES):
                load(0, t)
            iteration(0, ffn=False, tail=False)
            iteration(1, ffn=False, tail=False)
            iteration(2, tail=False)
            with sp.Fori(3, GROUPS - 1) as n:
                iteration(n)
            iteration(GROUPS - 1, loads=False)
            iteration(GROUPS, loads=False)
            iteration(GROUPS + 1, loads=False)
            send(GROUPS - 1, 1)
            for half in range(2):
                sp.wait_ge(out_sent[half], 16 * GROUPS)

        @block.vector
        def _(dve):
            def reduce_half(n, slot):
                t, half = divmod(slot, 2)
                if half == 0:
                    dve.wait_ge(x_landed[t], 16 * n + 16)
                    if not first(n):
                        dve.wait_ge(pool_summed, 2 * n - 1 if t < TILES - 1 else 2 * n)
                rows = xs[:, t, 7 * half:7 * half + 7, :].rearrange("p i (j k) -> p (i j) k", k=PATCH)
                dve.tensor_reduce(pooled[:, t, HALF * half:HALF * (half + 1)], rows, AX.X,
                                  ALU.add).then_inc(reduced, 1)

            def statistics(m, norm, width):
                at = 8 * m + 4 * norm
                if norm == 0:
                    dve.wait_ge(p_tok_ready, m + 1)
                    gram = ps[0:HALF, 1, :].rearrange("p (h g b r) -> p h g b r", h=2, g=2, b=GROUP)[:, :, 1]
                else:
                    dve.wait_ge(g2_summed, m + 1)
                    gram = ps[0:HALF, 1, 0:256].rearrange("p (h b r) -> p h b r", h=2, b=GROUP)
                for h in range(2):
                    last = dve.tensor_tensor(prod[:, h, :, 0:width], u_tok[:, h, :, 0:width],
                                             gram[:, h, :, 0:width], ALU.mult)
                last.then_inc(stat_steps, 1)
                dve.wait_ge(stat_steps, at + 1)
                dve.tensor_reduce(stat[:, 0, :], prod[:, :, :, 0:width].rearrange("p h b r -> p (h b) r"),
                                  AX.X, ALU.add).then_inc(stat_steps, 1)
                dve.wait_ge(stat_steps, at + 2)
                dve.tensor_scalar(stat[:, 1, :], stat[:, 0, :], EPS, None, ALU.add).then_inc(stat_steps, 1)
                dve.wait_ge(stat_steps, at + 3)
                dve.tensor_scalar(stat[:, 3, :], stat[:, 1, :], -0.5, None, ALU.mult)
                dve.tensor_scalar(stat[:, 2, :].bitcast(I32), stat[:, 1, :].bitcast(I32), -0.5, MAGIC,
                                  ALU.mult, ALU.add).then_inc(stat_steps, 1)

            def maxima(m):
                for b in range(GROUP):
                    dve.wait_ge(scores_ready, 4 * m + b + 1)
                    dve.tensor_reduce(neg_max[:, b, :],
                                      ps[0:HALF, b, 0:PAIR_TOKENS].rearrange("p (h k) -> p h k", h=2),
                                      AX.X, ALU.max, negate=True).then_inc(max_ready, 1)

            def context(m):
                dve.wait_ge(context_ready, m + 1)
                sums = ps[0:HALF, 1, 0:256].rearrange("p (h b r) -> p h b r", h=2, b=GROUP)
                dve.reciprocal(row_inv[:], sums[:, :, :, ONE_P]).then_inc(row_inv_ready, 1)
                dve.wait_ge(row_inv_ready, m + 1)
                for h in range(2):
                    last = dve.tensor_tensor(u_tok[:, h, :, CTX:ONE_U], sums[:, h, :, 0:CHANNELS],
                                             row_inv[:, h, :].unsqueeze(2).broadcast_to([HALF, GROUP, CHANNELS]),
                                             ALU.mult)
                last.then_inc(u_tok_ready, 1)

            def low_parts(f):
                dve.wait_ge(uhat_hi_ready, f + 1)
                if not first(f):
                    dve.wait_ge(hidden_summed, 12 * f)
                for k in range(2):
                    last = dve.scalar_tensor_tensor(
                        out=uhat_stack[:, PAIR_TOKENS * k:PAIR_TOKENS * (k + 1)],
                        in0=uhat_hi[:, PAIR_TOKENS * k:PAIR_TOKENS * (k + 1)].bitcast(F32),
                        scalar=cf[:, LO_ACT:LO_ACT + 1], in1=ps[:, 2 + k, 0:PAIR_TOKENS],
                        op0=ALU.mult, op1=ALU.add)
                last.then_inc(uhat_ready, 1)

            def setup_a():
                dve.wait_ge(cw_landed, 16)
                dve.tensor_reduce(cw_mean[:], cw_sb[:], AX.X, ALU.add, negate=True).then_inc(setup_dve, 1)
                dve.wait_ge(setup_dve, 1)
                dve.tensor_scalar(cw_mean[:], cw_mean[:], 1.0 / EMBED, None, ALU.mult).then_inc(setup_dve, 1)
                dve.wait_ge(setup_dve, 2)
                dve.tensor_scalar(cwc[:], cw_sb[:], cw_mean[:], None, ALU.add).then_inc(setup_dve, 1)
                dve.wait_ge(mix_landed, 32)
                dve.tensor_tensor(mix[:], alpha_sb[:, 0:1], alpha_sb[:, 1:2], ALU.mult).then_inc(setup_dve, 1)
                dve.wait_ge(setup_dve, 4)
                dve.wait_ge(cr_landed, 16)
                dve.tensor_scalar(mix_in[:], cr[0:MIXES, ROW_IN:ROW_IN + EMBED], mix[:], None,
                                  ALU.mult).then_inc(setup_dve, 1)

            def setup_b():
                dve.wait_ge(cf_landed, 16)
                dve.wait_ge(setup_pe, PE_G1)
                dve.tensor_tensor(id_g1[:, 128:256], ps[:, 0, 0:128], cf[:, MASK_G:MASK_G + 128], ALU.mult)
                dve.tensor_copy(id_g1[:, 0:128], ident).then_inc(setup_dve, 1)
                dve.wait_ge(setup_pe, PE_A)
                dve.tensor_tensor(score_mat[:], ps[:, 1, 0:128], cf[:, MASK_S:MASK_S + 128],
                                  ALU.mult).then_inc(setup_dve, 1)
                dve.wait_ge(wfc_landed, 32)
                dve.wait_ge(wproj_landed, 32)
                for k in range(2):
                    dve.tensor_tensor(bfc_sb[0:1, 384 * k:384 * (k + 1)], bfc_sb[0:1, 384 * k:384 * (k + 1)],
                                      ps[0:1, 4 + k, 0:384], ALU.mult)
                dve.tensor_tensor(bproj_sb[:], bproj_sb[:], ps[0:1, 6, 0:EMBED], ALU.mult).then_inc(setup_dve, 1)

            def setup_c():
                dve.wait_ge(setup_pe, PE_BASIS)
                dve.tensor_copy(resid[:], ps[:, 3, 256:256 + EMBED])
                dve.tensor_copy(basis_sb, ps[:, 3, 0:EMBED]).then_inc(setup_dve, 1)
                dve.wait_ge(setup_dve, 9)
                dve.tensor_reduce(basis_mean[:], basis_sb, AX.X, ALU.add, negate=True).then_inc(setup_dve, 1)
                dve.wait_ge(setup_dve, 10)
                dve.tensor_scalar(basis_mean[:], basis_mean[:], 1.0 / EMBED, None, ALU.mult).then_inc(setup_dve, 1)
                dve.wait_ge(setup_dve, 11)
                dve.tensor_scalar(basis_c, basis_sb, basis_mean[:], None, ALU.add).then_inc(setup_dve, 1)

            def setup_d():
                dve.wait_ge(setup_pe, PE_G2)
                dve.tensor_tensor(g2[:], ps[:, 0, 0:128], cf[:, MASK_G:MASK_G + 128], ALU.mult).then_inc(setup_dve, 1)

            def setup_e():
                dve.wait_ge(setup_act, ACT_FHI)
                for k in range(2):
                    last = dve.scalar_tensor_tensor(
                        out=f_stack[:, 384 * k:384 * (k + 1)], in0=f_hi[:, 384 * k:384 * (k + 1)].bitcast(F32),
                        scalar=cf[:, LO_W:LO_W + 1], in1=ps[:, 4 + k, 0:384], op0=ALU.mult, op1=ALU.add)
                last.then_inc(setup_dve, 1)

            def iteration(n, new=True, chain=True, ffn=True, setup={}):
                for slot in range(SLOTS):
                    if ffn and slot == 0:
                        low_parts(n - 2)
                    if new:
                        reduce_half(n, slot)
                    if slot in setup:
                        setup[slot]()
                    if chain and slot == 1:
                        statistics(n - 1, 0, CHANNELS)
                    if chain and slot == 5:
                        maxima(n - 1)
                    if chain and slot == 8:
                        context(n - 1)
                    if chain and slot == 10:
                        statistics(n - 1, 1, BASIS)

            iteration(0, chain=False, ffn=False, setup={0: setup_a, 2: setup_b, 4: setup_c, 6: setup_d, 8: setup_e})
            iteration(1, ffn=False)
            iteration(2)
            with dve.Fori(3, GROUPS) as n:
                iteration(n)
            iteration(GROUPS, new=False)
            iteration(GROUPS + 1, new=False, chain=False)

        @block.tensor
        def _(pe):
            def mm(o, a, b, start=True, stop=True):
                return pe.matmul(o, a, b, start=start, stop=stop)

            def setup():
                pe.wait_ge(cr_landed, 16)
                pe.wait_ge(setup_dve, 3)
                for k in range(2):
                    mm(ps[0:E2, 0, 128 * k:128 * (k + 1)], cwc[:, E2 * k:E2 * (k + 1)], cr[:, ROW_P:ROW_P + 128])
                for k in range(2):
                    last = mm(ps[0:E2, 0, 256 + 128 * k:256 + 128 * (k + 1)], cwc[:, E2 * k:E2 * (k + 1)],
                              cr[:, ROW_C:ROW_C + 128])
                last.then_inc(setup_pe, 1)
                pe.wait_ge(setup_act, ACT_CWT)
                pe.wait_ge(wqkv_landed, 32)
                for j in range(4):
                    o = ps[0:E2, 1, 128 * j:128 * (j + 1)]
                    for k in range(2):
                        mm(o, wqkv_sb[:, k, E2 * j:E2 * (j + 1)], cwt[:, k, :], k == 0, False)
                    last = mm(o, bqkv_sb[0:1, E2 * j:E2 * (j + 1)], cr[0:1, ROW_ONE_P:ROW_ONE_P + 128], False, True)
                last.then_inc(setup_pe, 1)
                pe.wait_ge(setup_dve, 5)
                for k in range(2):
                    for j in range(2):
                        mm(ps[0:E2, 2 + k if j == 0 else 6 + k, 0:384], mix_in[:, E2 * k:E2 * (k + 1)],
                           cr[0:MIXES, ROW_OUT + 384 * j:ROW_OUT + 384 * (j + 1)])
                for j in range(2):
                    last = mm(ps[0:1, 4 + j, 0:384], mix[:], cr[0:MIXES, ROW_OUT + 384 * j:ROW_OUT + 384 * (j + 1)])
                last.then_inc(setup_pe, 1)
                pe.wait_ge(setup_act, ACT_COEF)
                mm(ps[0:1, 6, 0:EMBED], mix[:], cr[0:MIXES, ROW_IN:ROW_IN + EMBED])
                pe.wait_ge(wfc_landed, 32)
                pe.wait_ge(cf_landed, 16)
                for k in range(2):
                    for t in range(4):
                        pe.transpose(ps[0:E2, 2 + k, 128 * t:128 * (t + 1)], wfc_sb[:, t, E2 * k:E2 * (k + 1)], ident)
                for k in range(2):
                    for t in range(4, HT):
                        last = pe.transpose(ps[0:E2, 7, 256 * k + 128 * (t - 4):256 * k + 128 * (t - 3)],
                                            wfc_sb[:, t, E2 * k:E2 * (k + 1)], ident)
                last.then_inc(setup_pe, 1)
                mm_g1()
                pe.wait_ge(setup_act, ACT_W0T)
                pe.wait_ge(setup_dve, 8)
                for at in (0, 256):
                    o = ps[:, 3, at:at + EMBED]
                    mm(o, cr[:, ROW_P:ROW_P + 128], cw_sb[:], True, False)
                    for k in range(2):
                        mm(o, cwt_ctx[:, k, :], wqkv_sb[:, k, 2 * EMBED:3 * EMBED], False, False)
                    last = mm(o, cr[0:1, ROW_ONE_U:ROW_ONE_U + 128], bqkv_sb[0:1, 2 * EMBED:3 * EMBED], False, at == 0)
                    if at:
                        last = mm(o, cr[0:1, ROW_ONE_U:ROW_ONE_U + 128], bproj_sb[0:1, :], False, True)
                last.then_inc(setup_pe, 1)
                pe.wait_ge(setup_dve, 12)
                for k in range(2):
                    last = pe.transpose(ps[0:E2, 2, 128 * k:128 * (k + 1)], basis_c[:, E2 * k:E2 * (k + 1)], ident)
                last.then_inc(setup_pe, 1)
                pe.wait_ge(setup_act, ACT_BT)
                for k in range(2):
                    last = mm(ps[:, 0, 0:128], basis_t[:, k, :], basis_t[:, k, :], k == 0, k == 1)
                last.then_inc(setup_pe, 1)
                pe.wait_ge(setup_pool, 1)
                for j in range(2):
                    o = ps[:, 4 + j, 0:384]
                    for k in range(2):
                        mm(o, basis_t[:, k, :], w0t[:, k, 384 * j:384 * (j + 1)], k == 0, False)
                    last = mm(o, cr[0:1, ROW_ONE_F:ROW_ONE_F + 128], bfc_sb[0:1, 384 * j:384 * (j + 1)], False, True)
                last.then_inc(setup_pe, 1)
                pe.wait_ge(setup_pool, 2)
                for t in range(HT):
                    for k in range(2):
                        at = EMBED * (t % 2) + E2 * k
                        last = pe.transpose(ps[:, (1, 6, 7)[t // 2], at:at + E2], wproj_sb[:, k, 128 * t:128 * (t + 1)],
                                            ident[0:E2, 0:E2])
                last.then_inc(setup_pe, 1)

            def mm_g1():
                for k in range(2):
                    last = mm(ps[:, 0, 0:128], cwt[:, k, :], cwt[:, k, :], k == 0, k == 1)
                last.then_inc(setup_pe, 1)
                for j in range(2):
                    last = mm(ps[:, 1, 0:128], qkt[:, 2 + j, :], qkt[:, j, :], j == 0, j == 1)
                last.then_inc(setup_pe, 1)

            def sum_rows(n, tiles):
                for t in tiles:
                    pe.wait_ge(reduced, SLOTS * n + 2 * t + 2)
                    last = mm(ps[:, 0, 0:TOKENS], cf[:, SEL_AT + 128 * t:SEL_AT + 128 * (t + 1)], pooled[:, t, :],
                              t == 0, t == TILES - 1)
                last.then_inc(pool_summed, 1)

            def to_tokens(m):
                pe.wait_ge(p_rows_ready, m + 1)
                for h in range(2):
                    last = mm(ps[0:HALF, 1, 256 * h:256 * (h + 1)], p_rows[:, HALF * h:HALF * (h + 1)], id_g1[:])
                last.then_inc(tok_summed, 1)

            def turn_phat(m):
                pe.wait_ge(phat_tok_ready, 2 * m + 2)
                if not first(m):
                    pe.wait_ge(uhat_ready, m)
                for h in range(2):
                    last = pe.transpose(ps[:, 2, HALF * h:HALF * (h + 1)],
                                        phat_tok[:, h].rearrange("p b r -> p (b r)"), ident[0:HALF, 0:HALF])
                last.then_inc(phat_turned, 1)

            def apply_a(m):
                pe.wait_ge(phat_rows_ready, m + 1)
                mm(ps[:, 3, 0:TOKENS], score_mat[:], phat_rows[:]).then_inc(b_summed, 1)

            def scores(m):
                pe.wait_ge(b_rows_ready, m + 1)
                for h in range(2):
                    for b in range(GROUP):
                        last = mm(ps[0:HALF, b, TOKENS * h:TOKENS * (h + 1)],
                                  phat_rows[Q * b:Q * (b + 1), HALF * h:HALF * (h + 1)], b_rows[Q * b:Q * (b + 1), :])
                        if h == 1:
                            last.then_inc(scores_ready, 1)

            def turn_probs(m):
                for b in range(GROUP):
                    pe.wait_ge(probs_ready, 4 * m + b + 1)
                    for k in range(2):
                        for h in range(2):
                            at = TOKENS * k + HALF * h
                            last = pe.transpose(ps[0:HALF, b, at:at + HALF],
                                                probs[:, b, h, HALF * k:HALF * (k + 1)], ident[0:HALF, 0:HALF])
                    last.then_inc(probs_turned, 1)

            def weigh(m):
                pe.wait_ge(probs_t_ready, 4 * m + 4)
                for h in range(2):
                    for b in range(GROUP):
                        at = 128 * h + Q * b
                        for k in range(2):
                            last = mm(ps[0:HALF, 1, at:at + ONE_P + 1], probs_t[:, b, k, HALF * h:HALF * (h + 1)],
                                      phat_tok[:, k, b, 0:ONE_P + 1], k == 0, k == 1)
                last.then_inc(context_ready, 1)

            def turn_u(m):
                pe.wait_ge(u_tok_ready, m + 1)
                for h in range(2):
                    last = pe.transpose(ps[:, 0, HALF * h:HALF * (h + 1)],
                                        u_tok[:, h].rearrange("p b r -> p (b r)"), ident[0:HALF, 0:HALF])
                last.then_inc(u_turned, 1)

            def apply_g2(m):
                pe.wait_ge(u_rows_ready, m + 1)
                for h in range(2):
                    last = mm(ps[0:HALF, 1, 128 * h:128 * (h + 1)], u_rows[:, HALF * h:HALF * (h + 1)], g2[:])
                last.then_inc(g2_summed, 1)

            def turn_uhat(m):
                pe.wait_ge(uhat_tok_ready, 2 * m + 2)
                for b in range(GROUP):
                    for h in range(2):
                        at = TOKENS * (b % 2) + HALF * h
                        last = pe.transpose(ps[:, 2 + b // 2, at:at + HALF],
                                            uhat_tok[:, h, b].rearrange("p c r -> p (c r)"),
                                            ident[0:HALF, 0:HALF])
                last.then_inc(uhat_turned, 1)

            def hidden(f, unit):
                if unit == 0:
                    pe.wait_ge(uhat_ready, f + 1)
                if not (first(f) and unit < 2):
                    pe.wait_ge(gelu_done, 12 * f + unit - 1)
                half, t = divmod(unit, HT)
                mm(ps[:, HB + unit % 2, 0:PAIR_TOKENS], f_stack[:, 128 * t:128 * (t + 1)],
                   uhat_stack[:, PAIR_TOKENS * half:PAIR_TOKENS * (half + 1)]).then_inc(hidden_summed, 1)

            def project(f, half, part):
                for r in range(4 * part, 4 * part + 4):
                    tile, t = divmod(r, HT)
                    b, h = 2 * half + tile // 2, tile % 2
                    o = ps[0:HALF, OB + tile % 2, 0:EMBED]
                    if t == 0:
                        if not (first(f) and half == 0 and tile < 2):
                            pe.wait_ge(out_ready, 8 * f + 4 * half + tile - 1)
                        pe.wait_ge(u_kept_ready, 2 * f + half + 1)
                        mm(o, u_kept[Q * b:Q * (b + 1), HALF * h:HALF * (h + 1)], resid[Q * b:Q * (b + 1), :],
                           True, False)
                    if tile == 0:
                        pe.wait_ge(h_lo_ready, 12 * f + HT * half + t + 1)
                    at = slice(HALF * tile, HALF * (tile + 1))
                    mm(o, h_hi[:, half, t, at], w1_hi[:, t, :], False, False)
                    mm(o, h_hi[:, half, t, at], w1_lo[:, t, :], False, False)
                    last = mm(o, h_lo[:, half, t, at], w1_hi[:, t, :], False, t == HT - 1)
                    if t == HT - 1:
                        last.then_inc(out_summed, 1)

            UNITS = {0: (0, 1), 1: (2,), 2: (3,), 3: (4,), 4: (5,), 5: (6, 7), 7: (8,), 8: (9,), 9: (10, 11)}

            def iteration(n, new=True, chain=True, ffn=True, tail=True):
                m, f = n - 1, n - 2
                for slot in range(SLOTS):
                    if chain:
                        if slot == 0:
                            sum_rows(m, [TILES - 1])
                        if slot == 1:
                            to_tokens(m)
                        if slot == 3:
                            apply_a(m)
                        if slot == 4:
                            scores(m)
                        if slot == 9:
                            turn_u(m)
                    if ffn and slot < 6 and slot in UNITS:
                        for unit in UNITS[slot]:
                            hidden(f, unit)
                    if slot < 6 and tail:
                        project(f - 1, 1, slot)
                    if slot >= 6 and ffn:
                        project(f, 0, slot - 6)
                    if chain:
                        if slot == 2:
                            turn_phat(m)
                        if slot == 6:
                            turn_probs(m)
                        if slot == 7:
                            weigh(m)
                        if slot == 9:
                            apply_g2(m)
                    if ffn and slot >= 6 and slot in UNITS:
                        for unit in UNITS[slot]:
                            hidden(f, unit)
                    if slot == SLOTS - 1:
                        if chain:
                            turn_uhat(m)
                        if new:
                            sum_rows(n, range(TILES - 1))

            setup()
            pe.wait_ge(setup_dve, 14)
            pe.wait_ge(setup_act, ACT_W1)
            pe.wait_ge(setup_pool, 4)
            iteration(0, chain=False, ffn=False, tail=False)
            iteration(1, ffn=False, tail=False)
            iteration(2, tail=False)
            with pe.Fori(3, GROUPS) as n:
                iteration(n)
            iteration(GROUPS, new=False)
            iteration(GROUPS + 1, new=False, chain=False)
            for part in range(6):
                project(GROUPS - 1, 1, part)

        @block.scalar
        def _(act):
            def setup():
                act.wait_ge(setup_pe, PE_CWT)
                act.copy(cwt[:], ps[0:E2, 0, 0:256].rearrange("p (k c) -> p k c", k=2))
                act.copy(cwt_ctx[:], ps[0:E2, 0, 256:512].rearrange("p (k c) -> p k c", k=2)).then_inc(setup_act, 1)
                act.wait_ge(setup_pe, PE_QKT)
                act.copy(qkt[:], ps[0:E2, 1, :].rearrange("p (j c) -> p j c", j=4)).then_inc(setup_act, 1)
                act.wait_ge(setup_pe, PE_COEF)
                act.copy(coef[:, :, 0:384], ps[0:E2, 2:4, 0:384])
                act.copy(coef[:, :, 384:768], ps[0:E2, 6:8, 0:384]).then_inc(setup_act, 1)
                act.wait_ge(setup_pe, PE_W0T)
                act.copy(w0t[:, :, 0:512], ps[0:E2, 2:4, :]).then_inc(setup_act, 1)
                act.copy(w0t[:, :, 512:768],
                         ps[0:E2, 7, :].rearrange("p (k c) -> p k c", k=2)).then_inc(setup_act, 1)
                act.wait_ge(setup_pe, PE_BT)
                act.copy(basis_t[:], ps[0:E2, 2, 0:256].rearrange("p (k c) -> p k c", k=2)).then_inc(setup_act, 1)
                act.wait_ge(setup_pe, PE_F)
                act.copy(f_hi.rearrange("p (k c) -> p k c", k=2), ps[:, 4:6, 0:384]).then_inc(setup_act, 1)
                act.wait_ge(setup_pe, PE_W1)
                act.copy(w1_f32[:, 0:2, :], ps[:, 1, 0:384].rearrange("p (t e) -> p t e", t=2))
                act.copy(w1_f32[:, 2:6, :].rearrange("p (a t) e -> p a (t e)", a=2), ps[:, 6:8, 0:384])
                act.copy(w1_hi[:, 0:2, :], ps[:, 1, 0:384].rearrange("p (t e) -> p t e", t=2))
                act.copy(w1_hi[:, 2:6, :].rearrange("p (a t) e -> p a (t e)", a=2),
                         ps[:, 6:8, 0:384]).then_inc(setup_act, 1)

            def copy_p(m):
                act.wait_ge(pool_summed, 2 * m + 2)
                act.copy(p_rows[:], ps[:, 0, 0:TOKENS]).then_inc(p_rows_ready, 1)

            def copy_p_tok(m):
                act.wait_ge(tok_summed, m + 1)
                if not first(m):
                    act.wait_ge(uhat_tok_ready, 2 * m)
                p = ps[0:HALF, 1, :].rearrange("p (h g b r) -> p h g b r", h=2, g=2, b=GROUP)
                for h in range(2):
                    last = act.copy(u_tok[:, h, :, 0:CHANNELS], p[:, h, 0, :, 0:CHANNELS])
                last.then_inc(p_tok_ready, 1)

            def copy_phat(m):
                act.wait_ge(phat_turned, m + 1)
                act.copy(phat_rows[:], ps[:, 2, 0:TOKENS]).then_inc(phat_rows_ready, 1)

            def copy_b(m):
                act.wait_ge(b_summed, m + 1)
                act.copy(b_rows[:], ps[:, 3, 0:TOKENS]).then_inc(b_rows_ready, 1)

            def exponentials(m):
                for b in range(GROUP):
                    act.wait_ge(max_ready, 4 * m + b + 1)
                    for h in range(2):
                        last = act.activation(probs[:, b, h, :], ps[0:HALF, b, TOKENS * h:TOKENS * (h + 1)], ACT.Exp,
                                              bias=neg_max[:, b, h:h + 1])
                    last.then_inc(probs_ready, 1)

            def copy_probs(m):
                for b in range(GROUP):
                    act.wait_ge(probs_turned, 4 * m + b + 1)
                    act.copy(probs_t[:, b].rearrange("p k q -> p (k q)"),
                             ps[0:HALF, b, 0:PAIR_TOKENS]).then_inc(probs_t_ready, 1)

            def copy_u(m):
                act.wait_ge(u_turned, m + 1)
                if not first(m):
                    act.wait_ge(u_kept_ready, 2 * m)
                act.copy(u_rows[:], ps[:, 0, 0:TOKENS]).then_inc(u_rows_ready, 1)

            def copy_uhat(m):
                act.wait_ge(uhat_turned, m + 1)
                act.copy(uhat_hi[:].rearrange("p (k c) -> p k c", k=2),
                         ps[:, 2:4, 0:PAIR_TOKENS]).then_inc(uhat_hi_ready, 1)

            def gelu(f, unit):
                half, t = divmod(unit, HT)
                act.wait_ge(hidden_summed, 12 * f + unit + 1)
                if not (first(f) and unit < 2):
                    act.wait_ge(h_lo_ready, 12 * f + unit - 1)
                if t == 0 and not first(f):
                    act.wait_ge(out_summed, 8 * f - 4 + 4 * half)
                summed = ps[:, HB + unit % 2, 0:PAIR_TOKENS]
                act.activation(h_f32[:, unit % 2, :], summed, ACT.Gelu_apprx_tanh)
                act.activation(h_hi[:, half, t, :], summed, ACT.Gelu_apprx_tanh).then_inc(gelu_done, 1)

            def take_out(f, half, tile):
                act.wait_ge(out_summed, 8 * f + 4 * half + tile + 1)
                if tile == 0 and not first(f):
                    act.wait_ge(out_sent[half], 16 * f)
                act.copy(out_sb[0:HALF, half, tile, :], ps[0:HALF, OB + tile % 2, 0:EMBED]).then_inc(out_ready, 1)

            UNITS = {0: (0,), 1: (1,), 2: (2,), 3: (3,), 4: (4, 5), 7: (6, 7), 8: (8,), 9: (9, 10), 10: (11,)}
            TAKES = {2: 0, 3: 1, 5: 2, 6: 3}
            CHAIN = {0: copy_p, 1: copy_p_tok, 2: copy_phat, 3: copy_b, 5: exponentials, 6: copy_probs, 9: copy_u,
                     11: copy_uhat}

            def iteration(n, chain=True, ffn=True, tail=True, before=True):
                m, f = n - 1, n - 2
                for slot in range(SLOTS):
                    if slot == 0 and before:
                        take_out(f - 1, 0, 3)
                    if slot in TAKES and tail:
                        take_out(f - 1, 1, TAKES[slot])
                    if slot - 6 in TAKES and ffn:
                        take_out(f, 0, TAKES[slot - 6])
                    late = slot in (9,)
                    if chain and slot in CHAIN and late:
                        CHAIN[slot](m)
                    if ffn and slot in UNITS:
                        for unit in UNITS[slot]:
                            gelu(f, unit)
                    if chain and slot in CHAIN and not late:
                        CHAIN[slot](m)

            setup()
            iteration(1, ffn=False, tail=False, before=False)
            iteration(2, tail=False, before=False)
            with act.Fori(3, GROUPS) as n:
                iteration(n)
            iteration(GROUPS)
            iteration(GROUPS + 1, chain=False)
            take_out(GROUPS - 1, 0, 3)
            for tile in range(4):
                take_out(GROUPS - 1, 1, tile)

        @block.gpsimd
        def _(pool):
            def setup():
                pool.memset(phat_tok[:], 0.0).then_inc(setup_pool_self, 1)
                pool.memset(u_tok[:], 0.0).then_inc(setup_pool_self, 1)
                pool.memset(uhat_tok[:], 0.0).then_inc(setup_pool_self, 1)
                pool.wait_ge(setup_pool_self, 3)
                pool.memset(phat_tok[:, :, :, ONE_P:ONE_P + 1], 1.0).then_inc(setup_pool_self, 1)
                pool.memset(u_tok[:, :, :, ONE_U:ONE_U + 1], 1.0).then_inc(setup_pool_self, 1)
                pool.memset(uhat_tok[:, :, :, :, ONE_F:ONE_F + 1].rearrange("p h b c r -> p (h b) c r"), 1.0).then_inc(setup_pool_self, 1)
                pool.wait_ge(setup_act, ACT_W0T)
                pool.tensor_tensor(w0t, w0t, coef, ALU.mult).then_inc(setup_pool, 1)
                pool.wait_ge(wproj_landed, 32)
                pool.tensor_tensor(wproj_sb[:], wproj_sb[:], coef, ALU.mult).then_inc(setup_pool, 1)
                pool.wait_ge(setup_act, ACT_W1)
                pool.tensor_tensor(w1_lo[:], w1_f32[:], w1_hi[:].bitcast(F32), ALU.subtract).then_inc(setup_pool, 1)
                pool.wait_ge(setup_pool_self, 6)
                pool.memset(zero[:], 0.0).then_inc(setup_pool_self, 1)
                pool.memset(three_halves[:], 1.5).then_inc(setup_pool, 1)
                pool.wait_ge(setup_pool, 4)
                pool.wait_ge(setup_pool_self, 7)

            inv_std = stat[:, 2, :].rearrange("p (h b) -> p h b", h=2)

            def inverse_root(m, norm):
                at = 24 * m + 12 * norm
                pool.wait_ge(stat_steps, 8 * m + 4 * norm + 4)
                h, y = stat[:, 3, :], stat[:, 2, :]
                for step in range(3):
                    pool.tensor_tensor(newton[:], y, y, ALU.mult).then_inc(newton_steps, 1)
                    pool.wait_ge(newton_steps, at + 4 * step + 1)
                    pool.tensor_tensor(newton[:], newton[:], h, ALU.mult).then_inc(newton_steps, 1)
                    pool.wait_ge(newton_steps, at + 4 * step + 2)
                    pool.tensor_tensor(newton[:], newton[:], three_halves[:], ALU.add).then_inc(newton_steps, 1)
                    pool.wait_ge(newton_steps, at + 4 * step + 3)
                    pool.tensor_tensor(y, y, newton[:], ALU.mult).then_inc(newton_steps, 1)
                    pool.wait_ge(newton_steps, at + 4 * step + 4)

            def scale_p():
                for h in range(2):
                    pool.tensor_tensor(phat_tok[:, h, :, 0:CHANNELS], u_tok[:, h, :, 0:CHANNELS],
                                       inv_std[:, h, :].unsqueeze(2).broadcast_to([HALF, GROUP, CHANNELS]),
                                       ALU.mult).then_inc(phat_tok_ready, 1)

            def scale_u():
                shape = [HALF, GROUP, 4, BASIS]
                for h in range(2):
                    pool.tensor_tensor(uhat_tok[:, h, :, :, 0:BASIS],
                                       u_tok[:, h, :, 0:BASIS].unsqueeze(2).broadcast_to(shape),
                                       inv_std[:, h, :].unsqueeze(2).unsqueeze(3).broadcast_to(shape),
                                       ALU.mult).then_inc(uhat_tok_ready, 1)

            def low_part(f, unit):
                half, t = divmod(unit, HT)
                pool.wait_ge(gelu_done, 12 * f + unit + 1)
                pool.tensor_tensor(h_lo[:, half, t, :], h_f32[:, unit % 2, :], h_hi[:, half, t, :].bitcast(F32),
                                   ALU.subtract).then_inc(h_lo_ready, 1)

            def keep_u(f, half):
                pool.wait_ge(u_rows_ready, f + 1)
                if not first(f):
                    pool.wait_ge(out_summed, 8 * f - 4 + 4 * half)
                if half == 1:
                    pool.wait_ge(h_lo_ready, 12 * f + HT)
                part = slice(64 * half, 64 * (half + 1))
                pool.tensor_tensor(u_kept[part, :], u_rows[part, :], zero[part, :].broadcast_to([64, TOKENS]),
                                   ALU.add).then_inc(u_kept_ready, 1)
                if half == 1:
                    pool.wait_ge(u_kept_ready, 2 * f + 2)

            def iteration(n, chain=True, ffn=True):
                m, f = n - 1, n - 2
                if ffn:
                    keep_u(f, 0)
                    low_part(f, 0)
                    low_part(f, 1)
                if chain:
                    inverse_root(m, 0)
                    scale_p()
                if ffn:
                    for unit in range(2, 6):
                        low_part(f, unit)
                    keep_u(f, 1)
                    for unit in range(6, 12):
                        low_part(f, unit)
                if chain:
                    inverse_root(m, 1)
                    scale_u()

            setup()
            iteration(1, ffn=False)
            iteration(2)
            with pool.Fori(3, GROUPS) as n:
                iteration(n)
            iteration(GROUPS)
            iteration(GROUPS + 1, chain=False)


def kernel(x, L0_tok_channel_weights, L0_attn_W_qkv, L0_attn_b_qkv, L0_ffn_w_fc, L0_ffn_b_fc, L0_ffn_w_proj,
           L0_ffn_b_proj, L0_ffn_alpha_e, L0_ffn_alpha_r):
    import concourse.bacc as bacc
    from concourse.bass_utils import run_bass_kernel_spmd

    full, rows = constants()
    arrays = {
        "x": x, "cw": L0_tok_channel_weights, "wqkv": L0_attn_W_qkv, "bqkv": L0_attn_b_qkv.reshape(1, -1),
        "wfc": L0_ffn_w_fc, "bfc": L0_ffn_b_fc.reshape(1, -1), "wproj": L0_ffn_w_proj,
        "bproj": L0_ffn_b_proj.reshape(1, -1),
        "alpha_e": np.repeat(L0_ffn_alpha_e, len(RATIO_CHOICES)).reshape(-1, 1),
        "alpha_r": np.tile(L0_ffn_alpha_r, len(EMBED_CHOICES)).reshape(-1, 1),
        "const_full": full, "const_rows": rows,
    }
    arrays = {k: np.ascontiguousarray(v) for k, v in arrays.items()}
    nc = bacc.Bacc("TRN2", target_bir_lowering=False, num_devices=1)
    args = [nc.dram_tensor(k, v.shape, F32, kind="ExternalInput").ap() for k, v in arrays.items()]
    out = nc.dram_tensor("out", (IMAGES, TOKENS, EMBED), F32, kind="ExternalOutput").ap()
    build(nc, *args, out)
    r = run_bass_kernel_spmd(nc, [arrays], core_ids=[0])
    return r.results[0]["out"]
```

```python
from contextlib import ExitStack

import numpy as np

import concourse.bass as bass
from concourse import mybir

F32 = mybir.dt.float32
F32R = mybir.dt.float32r
I32 = mybir.dt.int32
ALU = mybir.AluOpType
ACT = mybir.ActivationFunctionType
AX = mybir.AxisListType

IMAGES, CHANNELS, SIDE = 64, 12, 224
PATCH = 16
GRID = SIDE // PATCH
TOKENS = GRID * GRID
EMBED = 192
HIDDEN = 768
EPS = 1e-5
EMBED_CHOICES = (96, 144, 192)
RATIO_CHOICES = (2, 3, 4)
MIXES = len(EMBED_CHOICES) * len(RATIO_CHOICES)

GROUP = 4
GROUPS = IMAGES // GROUP
Q = 32
HALF = TOKENS // 2
PAIRS = 8
TILES = GROUP * CHANNELS // PAIRS
E2 = EMBED // 2
HT = HIDDEN // 128
PAIR_TOKENS = 2 * TOKENS

ONE_P = CHANNELS
CTX = CHANNELS
ONE_U = 2 * CHANNELS
BASIS = ONE_U + 1
ONE_F = BASIS

COLS = GROUP * CHANNELS
IMAGE_PAIR = 2 * CHANNELS
SEL_AT = 128
MASK_G = SEL_AT + TILES * IMAGE_PAIR
MASK_S, LO_ACT, LO_W = MASK_G + 128, MASK_G + 256, MASK_G + 257
FULL = LO_W + 1
ROW_P, ROW_C, ROW_ONE_U, ROW_ONE_P, ROW_ONE_F, ROW_IN = 0, 128, 256, 384, 512, 640
ROW_OUT = ROW_IN + EMBED
ROW_48 = ROW_OUT + HIDDEN
ROWS = ROW_48 + COLS
PAIR_MASK = TILES * 128
PAIRED = PAIR_MASK + COLS

SLOTS = 12
LAG = 5
MAGIC = float(0x5F3759DF)


def constants():
    full = np.zeros((128, FULL), np.float32)
    full[:, :128] = np.eye(128)
    for t in range(TILES):
        for p in range(128):
            b, c = divmod(PAIRS * t + p % PAIRS, CHANNELS)
            full[p, SEL_AT + IMAGE_PAIR * t + CHANNELS * (b % 2) + c] = 1.0
    block = np.kron(np.eye(GROUP), np.ones((Q, Q)))
    full[:, MASK_G:MASK_G + 128] = block / EMBED
    full[:, MASK_S:MASK_S + 128] = block / np.sqrt(EMBED)
    quadrant = np.arange(128) // Q
    full[:, LO_ACT] = -(quadrant % 2)
    full[:, LO_W] = -(quadrant // 2)
    rows = np.zeros((CHANNELS, ROWS), np.float32)
    for b in range(GROUP):
        for c in range(CHANNELS):
            rows[c, ROW_P + Q * b + c] = 1.0
            rows[c, ROW_C + Q * b + CTX + c] = 1.0
            rows[c, ROW_48 + CHANNELS * b + c] = 1.0
        rows[0, ROW_ONE_U + Q * b + ONE_U] = 1.0
        rows[0, ROW_ONE_P + Q * b + ONE_P] = 1.0
        rows[0, ROW_ONE_F + Q * b + ONE_F] = 1.0
    for i, e in enumerate(EMBED_CHOICES):
        for j, r in enumerate(RATIO_CHOICES):
            k = len(RATIO_CHOICES) * i + j
            rows[k, ROW_IN:ROW_IN + e] = 1.0
            rows[k, ROW_OUT:ROW_OUT + r * e] = 1.0
    paired = np.zeros((COLS, PAIRED), np.float32)
    for t in range(TILES):
        for p in range(128):
            paired[PAIRS * t + p % PAIRS, 128 * t + p] = 1.0
    paired[:, PAIR_MASK:] = np.kron(np.eye(GROUP), np.ones((CHANNELS, CHANNELS))) / EMBED
    return full, rows, paired


def build(nc, x, cw, wqkv, bqkv, wfc, bfc, wproj, bproj, alpha_e, alpha_r, const_full, const_rows, const_paired, out):
    with ExitStack() as ctx:
        def sb(name, shape, dt=F32):
            return ctx.enter_context(nc.sbuf_tensor(name, shape, dt))

        def sem(name):
            return ctx.enter_context(nc.semaphore(name))

        cf = sb("cf", [128, FULL])
        cr = sb("cr", [CHANNELS, ROWS])
        cw_sb = sb("cw_sb", [CHANNELS, EMBED])
        cw_mean = sb("cw_mean", [CHANNELS, 1])
        cwc = sb("cwc", [CHANNELS, EMBED])
        wqkv_sb = sb("wqkv_sb", [E2, 2, 3 * EMBED])
        bqkv_sb = sb("bqkv_sb", [1, 3 * EMBED])
        bfc_sb = sb("bfc_sb", [1, HIDDEN])
        wproj_sb = sb("wproj_sb", [E2, 2, HIDDEN])
        bproj_sb = sb("bproj_sb", [1, EMBED])
        alpha_sb = sb("alpha_sb", [MIXES, 2])
        mix = sb("mix", [MIXES, 1])
        mix_in = sb("mix_in", [MIXES, EMBED])
        cwt = sb("cwt", [E2, 2, 128])
        cwt_ctx = sb("cwt_ctx", [E2, 2, 128])
        cwt_48 = sb("cwt_48", [E2, 2, COLS])
        gram_48 = sb("gram_48", [COLS, COLS])
        qkt = sb("qkt", [E2, 4, 128])
        basis_mean = sb("basis_mean", [128, 1])
        basis_t = sb("basis_t", [E2, 2, 128])
        sel_gram = sb("sel_gram", [128, TILES, 2, IMAGE_PAIR])
        score_mat = sb("score_mat", [128, 128])
        g2 = sb("g2", [128, 128])
        resid = sb("resid", [128, EMBED])
        f_stack = sb("f_stack", [128, HIDDEN], F32R)
        w1_hi = sb("w1_hi", [128, HT, EMBED], F32R)
        w1_lo = sb("w1_lo", [128, HT, EMBED], F32R)
        xs = sb("xs", [128, TILES, GRID, SIDE])
        pooled = sb("pooled", [128, TILES, TOKENS])
        p_tok = sb("p_tok", [HALF, 2, GROUP, CHANNELS])
        p_kept = sb("p_kept", [HALF, 2, GROUP, CHANNELS])
        phat_kept = sb("phat_kept", [HALF, 2, GROUP, Q])
        context_rows = sb("context_rows", [128, TOKENS])
        u_tok = sb("u_tok", [HALF, 2, GROUP, Q])
        phat_tok = sb("phat_tok", [HALF, 2, GROUP, Q])
        uhat_tok = sb("uhat_tok", [HALF, 2, GROUP, 4, Q])
        prod = sb("prod", [HALF, 2, 2, GROUP, BASIS])
        stat = sb("stat", [HALF, 4, 2, 2 * GROUP])
        newton = sb("newton", [HALF, 2, 2 * GROUP])
        phat_rows = sb("phat_rows", [128, TOKENS])
        b_rows = sb("b_rows", [128, TOKENS])
        neg_max = sb("neg_max", [HALF, GROUP, 2])
        probs = sb("probs", [HALF, GROUP, 2, TOKENS])
        probs_t = sb("probs_t", [HALF, GROUP, 2, TOKENS])
        three_halves = sb("three_halves", [HALF, 2, 2 * GROUP])
        zero = sb("zero", [128, 1])
        row_inv = sb("row_inv", [HALF, 2, GROUP])
        u_rows = sb("u_rows", [128, TOKENS])
        u_kept = [sb("u_kept0", [128, TOKENS]), sb("u_kept1", [128, TOKENS])]
        uhat_hi = sb("uhat_hi", [128, GROUP * TOKENS], F32R)
        uhat_stack = sb("uhat_stack", [128, GROUP * TOKENS], F32R)
        h_f32 = sb("h_f32", [128, 4, PAIR_TOKENS])
        h_hi = sb("h_hi", [128, 2, HT, PAIR_TOKENS], F32R)
        h_lo = sb("h_lo", [128, 2, HT, PAIR_TOKENS], F32R)
        out_sb = sb("out_sb", [128, 2, GROUP, EMBED])
        w0t = probs[0:E2].rearrange("p b h k -> p (b h k)")[:, 0:2 * HIDDEN].rearrange("p (k h) -> p k h", k=2)
        coef = probs_t[0:E2].rearrange("p b k q -> p (b k q)")[:, 0:2 * HIDDEN].rearrange("p (k h) -> p k h", k=2)
        wfc_sb = out_sb[:].rearrange("p h b e -> p (h b) e")[:, 0:HT, :]
        paired_sb = h_f32[0:COLS].rearrange("p s c -> p (s c)")[:, 0:PAIRED]
        w1_f32 = h_f32[:].rearrange("p s c -> p (s c)")[:, 0:HT * EMBED].rearrange("p (t e) -> p t e", t=HT)
        basis_sb, basis_c = phat_rows[:, 0:EMBED], b_rows[:, 0:EMBED]
        f_hi = uhat_hi[:, 0:HIDDEN]

        ps = ctx.enter_context(nc.psum_tensor("ps", [128, 8, 512], F32))
        HB, OB = 4, 6

        x_landed = [sem(f"x_landed{t}") for t in range(TILES)]
        cf_landed = sem("cf_landed")
        cr_landed = sem("cr_landed")
        cw_landed = sem("cw_landed")
        wqkv_landed = sem("wqkv_landed")
        mix_landed = sem("mix_landed")
        wfc_landed = sem("wfc_landed")
        wproj_landed = sem("wproj_landed")
        setup_pe = sem("setup_pe")
        setup_act = sem("setup_act")
        setup_dve = sem("setup_dve")
        setup_pool = sem("setup_pool")
        setup_pool_self = sem("setup_pool_self")
        reduced = sem("reduced")
        pool_summed = sem("pool_summed")
        p_tok_ready = sem("p_tok_ready")
        stat_steps = sem("stat_steps")
        newton_steps = sem("newton_steps")
        phat_tok_ready = sem("phat_tok_ready")
        phat_turned = sem("phat_turned")
        phat_rows_ready = sem("phat_rows_ready")
        b_summed = sem("b_summed")
        b_rows_ready = sem("b_rows_ready")
        scores_ready = sem("scores_ready")
        max_ready = sem("max_ready")
        probs_ready = sem("probs_ready")
        probs_turned = sem("probs_turned")
        probs_t_ready = sem("probs_t_ready")
        context_summed = sem("context_summed")
        context_rows_ready = sem("context_rows_ready")
        context_ready = sem("context_ready")
        p_in_u_ready = sem("p_in_u_ready")
        p_kept_ready = sem("p_kept_ready")
        phat_kept_ready = sem("phat_kept_ready")
        row_inv_ready = sem("row_inv_ready")
        u_tok_ready = sem("u_tok_ready")
        u_turned = sem("u_turned")
        u_rows_ready = sem("u_rows_ready")
        g2_summed = sem("g2_summed")
        uhat_tok_ready = sem("uhat_tok_ready")
        uhat_turned = sem("uhat_turned")
        uhat_hi_ready = sem("uhat_hi_ready")
        uhat_ready = sem("uhat_ready")
        u_kept_ready = [sem("u_kept0_ready"), sem("u_kept1_ready")]
        hidden_summed = sem("hidden_summed")
        gelu_done = sem("gelu_done")
        h_lo_ready = sem("h_lo_ready")
        out_summed = sem("out_summed")
        out_ready = sem("out_ready")
        out_sent = [sem("out_sent0"), sem("out_sent1")]

        ident = cf[:, 0:128]
        x_tiles = x.rearrange("(n b) c (i k) w -> n k (b c) i w", b=GROUP, k=PATCH)
        out_tiles = out.rearrange("(n b) (h p) e -> n p b h e", b=2, h=2)

        PE_CWT, PE_QKT, PE_COEF, PE_W0T, PE_G1, PE_A, PE_BASIS, PE_BT, PE_G2, PE_F, PE_W1 = range(1, 12)
        ACT_CWT, ACT_QKT, ACT_COEF, ACT_ROWS, ACT_W0T, ACT_BT, ACT_FHI, ACT_W1 = range(1, 9)

        block = ctx.enter_context(nc.Block())

        def first(n):
            return isinstance(n, int) and n == 0

        def run(engine, iteration, start=0):
            for n in range(start, GROUPS + LAG):
                if n == LAG:
                    with engine.Fori(LAG, GROUPS) as i:
                        iteration(i, set(range(LAG + 1)))
                elif n < LAG or n >= GROUPS:
                    iteration(n, {k for k in range(LAG + 1) if 0 <= n - k < GROUPS})

        @block.sync
        def _(sp):
            def load(n, t):
                sp.dma_start(xs[:, t], x_tiles[n, :, PAIRS * t:PAIRS * (t + 1)]).then_inc(x_landed[t], 16)

            def reload(n, t):
                sp.wait_ge(reduced, SLOTS * (n - 1) + 2 * t + 2)
                load(n, t)

            def send(m, half):
                sp.wait_ge(out_ready, 8 * m + 4 * half + 4)
                sp.dma_start(out_tiles[2 * m + half],
                             out_sb[0:HALF, half].rearrange("p (b h) e -> p b h e", b=2)).then_inc(out_sent[half], 16)

            def iteration(n, on, loads=True):
                for t in range(TILES):
                    if loads:
                        reload(n + 1, t)
                    if t == 1 and 5 in on:
                        send(n - 5, 1)
                    if t == 4 and 4 in on:
                        send(n - 4, 0)

            load(0, 0)
            sp.dma_start(cr[:], const_rows).then_inc(cr_landed, 16)
            sp.dma_start(cw_sb[:], cw).then_inc(cw_landed, 16)
            sp.dma_start(cf[:], const_full).then_inc(cf_landed, 16)
            sp.dma_start(paired_sb, const_paired).then_inc(cf_landed, 16)
            sp.dma_start(alpha_sb[:, 0:1], alpha_e).then_inc(mix_landed, 16)
            sp.dma_start(alpha_sb[:, 1:2], alpha_r).then_inc(mix_landed, 16)
            sp.dma_start(bqkv_sb[:], bqkv).then_inc(wqkv_landed, 16)
            sp.dma_start(wqkv_sb[:], wqkv.rearrange("(k p) n -> p k n", k=2)).then_inc(wqkv_landed, 16)
            load(0, 1)
            sp.dma_start(bfc_sb[:], bfc).then_inc(wfc_landed, 16)
            sp.dma_start(wfc_sb, wfc.rearrange("(t p) e -> p t e", p=128)).then_inc(wfc_landed, 16)
            load(0, 2)
            sp.dma_start(bproj_sb[:], bproj).then_inc(wproj_landed, 16)
            sp.dma_start(wproj_sb[:], wproj.rearrange("(k p) h -> p k h", k=2)).then_inc(wproj_landed, 16)
            for t in range(3, TILES):
                load(0, t)
            for n in range(LAG):
                iteration(n, set(range(n + 1)))
            with sp.Fori(LAG, GROUPS - 1) as n:
                iteration(n, set(range(LAG + 1)))
            for n in range(GROUPS - 1, GROUPS + LAG):
                iteration(n, {k for k in range(LAG + 1) if n - k < GROUPS}, loads=False)
            for half in range(2):
                sp.wait_ge(out_sent[half], 16 * GROUPS)

        @block.vector
        def _(dve):
            def reduce_half(n, slot):
                t, half = divmod(slot, 2)
                if half == 0:
                    dve.wait_ge(x_landed[t], 16 * n + 16)
                    if not first(n):
                        dve.wait_ge(pool_summed, 2 * n - 1 if t < TILES // 2 else 2 * n)
                rows = xs[:, t, 7 * half:7 * half + 7, :].rearrange("p i (j k) -> p (i j) k", k=PATCH)
                dve.tensor_reduce(pooled[:, t, HALF * half:HALF * (half + 1)], rows, AX.X,
                                  ALU.add).then_inc(reduced, 1)

            def statistics(n, norm1, norm2):
                at = 4 * (n - 1)
                if norm1:
                    dve.wait_ge(p_tok_ready, n)
                    gram = ps[0:HALF, 0, 0:4 * COLS].rearrange("p (h g b r) -> p h g b r", h=2, g=2, b=GROUP)
                    for h in range(2):
                        last = dve.tensor_tensor(prod[:, 0, h, :, 0:CHANNELS], p_tok[:, h], gram[:, h, 1], ALU.mult)
                if norm2:
                    dve.wait_ge(g2_summed, n - 2)
                    gram2 = ps[0:HALF, 1, 0:256].rearrange("p (h b r) -> p h b r", h=2, b=GROUP)
                    for h in range(2):
                        last = dve.tensor_tensor(prod[:, 1, h], u_tok[:, h, :, 0:BASIS], gram2[:, h, :, 0:BASIS],
                                                 ALU.mult)
                last.then_inc(stat_steps, 1)
                dve.wait_ge(stat_steps, at + 1)
                if norm1:
                    last = dve.tensor_reduce(stat[:, 0, 0, :],
                                             prod[:, 0, :, :, 0:CHANNELS].rearrange("p h b r -> p (h b) r"),
                                             AX.X, ALU.add)
                if norm2:
                    last = dve.tensor_reduce(stat[:, 0, 1, :], prod[:, 1].rearrange("p h b r -> p (h b) r"),
                                             AX.X, ALU.add)
                last.then_inc(stat_steps, 1)
                dve.wait_ge(stat_steps, at + 2)
                dve.tensor_scalar(stat[:, 1], stat[:, 0], EPS, None, ALU.add).then_inc(stat_steps, 1)
                dve.wait_ge(stat_steps, at + 3)
                dve.tensor_scalar(stat[:, 3], stat[:, 1], -0.5, None, ALU.mult)
                dve.tensor_scalar(stat[:, 2].bitcast(I32), stat[:, 1].bitcast(I32), -0.5, MAGIC,
                                  ALU.mult, ALU.add).then_inc(stat_steps, 1)

            def maxima(m):
                for b in range(GROUP):
                    dve.wait_ge(scores_ready, 4 * m + b + 1)
                    dve.tensor_reduce(neg_max[:, b, :],
                                      ps[0:HALF, b, 0:PAIR_TOKENS].rearrange("p (h k) -> p h k", h=2),
                                      AX.X, ALU.max, negate=True).then_inc(max_ready, 1)

            def context(m):
                dve.wait_ge(context_ready, m + 1)
                sums = ps[0:HALF, 1, 256:512].rearrange("p (h b r) -> p h b r", h=2, b=GROUP)
                dve.reciprocal(row_inv[:], sums[:, :, :, ONE_P]).then_inc(row_inv_ready, 1)
                dve.wait_ge(row_inv_ready, m + 1)
                for h in range(2):
                    last = dve.tensor_tensor(u_tok[:, h, :, CTX:ONE_U], sums[:, h, :, 0:CHANNELS],
                                             row_inv[:, h, :].unsqueeze(2).broadcast_to([HALF, GROUP, CHANNELS]),
                                             ALU.mult)
                last.then_inc(u_tok_ready, 1)

            def low_parts(f):
                dve.wait_ge(uhat_hi_ready, f + 1)
                if not first(f):
                    dve.wait_ge(hidden_summed, 12 * f)
                for k in range(2):
                    last = dve.scalar_tensor_tensor(
                        out=uhat_stack[:, PAIR_TOKENS * k:PAIR_TOKENS * (k + 1)],
                        in0=uhat_hi[:, PAIR_TOKENS * k:PAIR_TOKENS * (k + 1)].bitcast(F32),
                        scalar=cf[:, LO_ACT:LO_ACT + 1], in1=ps[:, 2 + k, 0:PAIR_TOKENS],
                        op0=ALU.mult, op1=ALU.add)
                last.then_inc(uhat_ready, 1)

            def setup_a():
                dve.wait_ge(cw_landed, 16)
                dve.tensor_reduce(cw_mean[:], cw_sb[:], AX.X, ALU.add, negate=True).then_inc(setup_dve, 1)
                dve.wait_ge(setup_dve, 1)
                dve.tensor_scalar(cw_mean[:], cw_mean[:], 1.0 / EMBED, None, ALU.mult).then_inc(setup_dve, 1)
                dve.wait_ge(setup_dve, 2)
                dve.tensor_scalar(cwc[:], cw_sb[:], cw_mean[:], None, ALU.add).then_inc(setup_dve, 1)
                dve.wait_ge(mix_landed, 32)
                dve.tensor_tensor(mix[:], alpha_sb[:, 0:1], alpha_sb[:, 1:2], ALU.mult).then_inc(setup_dve, 1)
                dve.wait_ge(setup_dve, 4)
                dve.wait_ge(cr_landed, 16)
                dve.tensor_scalar(mix_in[:], cr[0:MIXES, ROW_IN:ROW_IN + EMBED], mix[:], None,
                                  ALU.mult).then_inc(setup_dve, 1)

            def setup_b():
                dve.wait_ge(cf_landed, 32)
                dve.wait_ge(setup_pe, PE_G1)
                dve.tensor_tensor(gram_48[:], ps[0:COLS, 0, 0:COLS], paired_sb[:, PAIR_MASK:], ALU.mult)
                dve.tensor_copy(sel_gram[:, :, 0, :], cf[:, SEL_AT:MASK_G].rearrange("p (t c) -> p t c", t=TILES)
                                ).then_inc(setup_dve, 1)
                dve.wait_ge(setup_pe, PE_A)
                dve.tensor_tensor(score_mat[:], ps[:, 1, 0:128], cf[:, MASK_S:MASK_S + 128],
                                  ALU.mult).then_inc(setup_dve, 1)
                dve.wait_ge(wfc_landed, 32)
                dve.wait_ge(wproj_landed, 32)
                for k in range(2):
                    dve.tensor_tensor(bfc_sb[0:1, 384 * k:384 * (k + 1)], bfc_sb[0:1, 384 * k:384 * (k + 1)],
                                      ps[0:1, 4 + k, 0:384], ALU.mult)
                dve.tensor_tensor(bproj_sb[:], bproj_sb[:], ps[0:1, 6, 0:EMBED], ALU.mult).then_inc(setup_dve, 1)

            def setup_c():
                dve.wait_ge(setup_pe, PE_BASIS)
                dve.tensor_copy(resid[:], ps[:, 3, 256:256 + EMBED])
                dve.tensor_copy(basis_sb, ps[:, 3, 0:EMBED]).then_inc(setup_dve, 1)
                dve.wait_ge(setup_dve, 9)
                dve.tensor_reduce(basis_mean[:], basis_sb, AX.X, ALU.add, negate=True).then_inc(setup_dve, 1)
                dve.wait_ge(setup_dve, 10)
                dve.tensor_scalar(basis_mean[:], basis_mean[:], 1.0 / EMBED, None, ALU.mult).then_inc(setup_dve, 1)
                dve.wait_ge(setup_dve, 11)
                dve.tensor_scalar(basis_c, basis_sb, basis_mean[:], None, ALU.add).then_inc(setup_dve, 1)

            def setup_d():
                dve.wait_ge(setup_pe, PE_G2)
                dve.tensor_tensor(g2[:], ps[:, 0, 0:128], cf[:, MASK_G:MASK_G + 128], ALU.mult).then_inc(setup_dve, 1)

            def setup_e():
                dve.wait_ge(setup_act, ACT_FHI)
                for k in range(2):
                    last = dve.scalar_tensor_tensor(
                        out=f_stack[:, 384 * k:384 * (k + 1)], in0=f_hi[:, 384 * k:384 * (k + 1)].bitcast(F32),
                        scalar=cf[:, LO_W:LO_W + 1], in1=ps[:, 4 + k, 0:384], op0=ALU.mult, op1=ALU.add)
                last.then_inc(setup_dve, 1)

            SETUP = {0: setup_a, 2: setup_b, 4: setup_c, 6: setup_d, 8: setup_e}

            def iteration(n, on):
                for slot in range(SLOTS):
                    if 0 in on:
                        reduce_half(n, slot)
                    if first(n) and slot in SETUP:
                        SETUP[slot]()
                    if slot == 2 and (1 in on or 3 in on):
                        statistics(n, 1 in on, 3 in on)
                    if slot == 4 and 2 in on:
                        maxima(n - 2)
                    if slot == 9 and 3 in on:
                        low_parts(n - 3)
                    if slot == 11 and 2 in on:
                        context(n - 2)

            run(dve, iteration)

        @block.tensor
        def _(pe):
            def mm(o, a, b, start=True, stop=True):
                return pe.matmul(o, a, b, start=start, stop=stop)

            def setup():
                pe.wait_ge(cr_landed, 16)
                pe.wait_ge(setup_dve, 3)
                for k in range(2):
                    mm(ps[0:E2, 0, 128 * k:128 * (k + 1)], cwc[:, E2 * k:E2 * (k + 1)], cr[:, ROW_P:ROW_P + 128])
                for k in range(2):
                    last = mm(ps[0:E2, 0, 256 + 128 * k:256 + 128 * (k + 1)], cwc[:, E2 * k:E2 * (k + 1)],
                              cr[:, ROW_C:ROW_C + 128])
                for k in range(2):
                    last = mm(ps[0:E2, 2, COLS * k:COLS * (k + 1)], cwc[:, E2 * k:E2 * (k + 1)],
                              cr[:, ROW_48:ROW_48 + COLS])
                last.then_inc(setup_pe, 1)
                pe.wait_ge(setup_act, ACT_CWT)
                pe.wait_ge(wqkv_landed, 32)
                for j in range(4):
                    o = ps[0:E2, 1, 128 * j:128 * (j + 1)]
                    for k in range(2):
                        mm(o, wqkv_sb[:, k, E2 * j:E2 * (j + 1)], cwt[:, k, :], k == 0, False)
                    last = mm(o, bqkv_sb[0:1, E2 * j:E2 * (j + 1)], cr[0:1, ROW_ONE_P:ROW_ONE_P + 128], False, True)
                last.then_inc(setup_pe, 1)
                pe.wait_ge(setup_dve, 5)
                for k in range(2):
                    for j in range(2):
                        mm(ps[0:E2, 2 + k if j == 0 else 6 + k, 0:384], mix_in[:, E2 * k:E2 * (k + 1)],
                           cr[0:MIXES, ROW_OUT + 384 * j:ROW_OUT + 384 * (j + 1)])
                for j in range(2):
                    last = mm(ps[0:1, 4 + j, 0:384], mix[:], cr[0:MIXES, ROW_OUT + 384 * j:ROW_OUT + 384 * (j + 1)])
                last.then_inc(setup_pe, 1)
                pe.wait_ge(setup_act, ACT_COEF)
                mm(ps[0:1, 6, 0:EMBED], mix[:], cr[0:MIXES, ROW_IN:ROW_IN + EMBED])
                pe.wait_ge(wfc_landed, 32)
                pe.wait_ge(cf_landed, 32)
                for k in range(2):
                    for t in range(4):
                        pe.transpose(ps[0:E2, 2 + k, 128 * t:128 * (t + 1)], wfc_sb[:, t, E2 * k:E2 * (k + 1)], ident)
                for k in range(2):
                    for t in range(4, HT):
                        last = pe.transpose(ps[0:E2, 7, 256 * k + 128 * (t - 4):256 * k + 128 * (t - 3)],
                                            wfc_sb[:, t, E2 * k:E2 * (k + 1)], ident)
                last.then_inc(setup_pe, 1)
                mm_g1()
                pe.wait_ge(setup_act, ACT_W0T)
                pe.wait_ge(setup_dve, 8)
                for t in range(TILES):
                    pair = t // (TILES // 2)
                    mm(ps[:, 1, IMAGE_PAIR * t:IMAGE_PAIR * (t + 1)], paired_sb[:, 128 * t:128 * (t + 1)],
                       gram_48[:, IMAGE_PAIR * pair:IMAGE_PAIR * (pair + 1)])
                for at in (0, 256):
                    o = ps[:, 3, at:at + EMBED]
                    mm(o, cr[:, ROW_P:ROW_P + 128], cw_sb[:], True, False)
                    for k in range(2):
                        mm(o, cwt_ctx[:, k, :], wqkv_sb[:, k, 2 * EMBED:3 * EMBED], False, False)
                    last = mm(o, cr[0:1, ROW_ONE_U:ROW_ONE_U + 128], bqkv_sb[0:1, 2 * EMBED:3 * EMBED], False, at == 0)
                    if at:
                        last = mm(o, cr[0:1, ROW_ONE_U:ROW_ONE_U + 128], bproj_sb[0:1, :], False, True)
                last.then_inc(setup_pe, 1)
                pe.wait_ge(setup_dve, 12)
                for k in range(2):
                    last = pe.transpose(ps[0:E2, 2, 128 * k:128 * (k + 1)], basis_c[:, E2 * k:E2 * (k + 1)], ident)
                last.then_inc(setup_pe, 1)
                pe.wait_ge(setup_act, ACT_BT)
                for k in range(2):
                    last = mm(ps[:, 0, 0:128], basis_t[:, k, :], basis_t[:, k, :], k == 0, k == 1)
                last.then_inc(setup_pe, 1)
                pe.wait_ge(setup_pool, 1)
                for j in range(2):
                    o = ps[:, 4 + j, 0:384]
                    for k in range(2):
                        mm(o, basis_t[:, k, :], w0t[:, k, 384 * j:384 * (j + 1)], k == 0, False)
                    last = mm(o, cr[0:1, ROW_ONE_F:ROW_ONE_F + 128], bfc_sb[0:1, 384 * j:384 * (j + 1)], False, True)
                last.then_inc(setup_pe, 1)
                pe.wait_ge(setup_pool, 2)
                for t in range(HT):
                    for k in range(2):
                        at = EMBED * (t % 2) + E2 * k
                        last = pe.transpose(ps[:, (1, 6, 7)[t // 2], at:at + E2], wproj_sb[:, k, 128 * t:128 * (t + 1)],
                                            ident[0:E2, 0:E2])
                last.then_inc(setup_pe, 1)

            def mm_g1():
                for k in range(2):
                    last = mm(ps[0:COLS, 0, 0:COLS], cwt_48[:, k, :], cwt_48[:, k, :], k == 0, k == 1)
                last.then_inc(setup_pe, 1)
                for j in range(2):
                    last = mm(ps[:, 1, 0:128], qkt[:, 2 + j, :], qkt[:, j, :], j == 0, j == 1)
                last.then_inc(setup_pe, 1)

            def sum_rows(n, pair):
                first_tile = TILES // 2 * pair
                if pair == 0 and not first(n):
                    pe.wait_ge(b_rows_ready, n)
                for t in range(first_tile, first_tile + TILES // 2):
                    pe.wait_ge(reduced, SLOTS * n + 2 * t + 2)
                for h in range(2):
                    o = ps[0:HALF, 0, 2 * COLS * h:2 * COLS * (h + 1)].rearrange("p (g c) -> p g c", g=2)[
                        :, :, IMAGE_PAIR * pair:IMAGE_PAIR * (pair + 1)]
                    for t in range(first_tile, first_tile + TILES // 2):
                        last = mm(o, pooled[:, t, HALF * h:HALF * (h + 1)], sel_gram[:, t], t == first_tile,
                                  t == first_tile + TILES // 2 - 1)
                last.then_inc(pool_summed, 1)

            def turn_phat(m):
                pe.wait_ge(phat_tok_ready, 2 * m + 2)
                for h in range(2):
                    last = pe.transpose(ps[:, 0, HALF * h:HALF * (h + 1)],
                                        phat_tok[:, h].rearrange("p b r -> p (b r)"), ident[0:HALF, 0:HALF])
                last.then_inc(phat_turned, 1)

            def apply_a(m):
                pe.wait_ge(phat_rows_ready, m + 1)
                mm(ps[:, 0, 0:TOKENS], score_mat[:], phat_rows[:]).then_inc(b_summed, 1)

            def scores(m):
                pe.wait_ge(b_rows_ready, m + 1)
                pe.wait_ge(stat_steps, 4 * (m + 1) + 1)
                for h in range(2):
                    for b in range(GROUP):
                        last = mm(ps[0:HALF, b, TOKENS * h:TOKENS * (h + 1)],
                                  phat_rows[Q * b:Q * (b + 1), HALF * h:HALF * (h + 1)], b_rows[Q * b:Q * (b + 1), :])
                        if h == 1:
                            last.then_inc(scores_ready, 1)

            def turn_probs(m):
                for b in range(GROUP):
                    pe.wait_ge(probs_ready, 4 * m + b + 1)
                    for k in range(2):
                        for h in range(2):
                            at = TOKENS * k + HALF * h
                            last = pe.transpose(ps[0:HALF, b, at:at + HALF],
                                                probs[:, b, h, HALF * k:HALF * (k + 1)], ident[0:HALF, 0:HALF])
                    last.then_inc(probs_turned, 1)

            def weigh(m):
                pe.wait_ge(phat_kept_ready, m + 1)
                for k in range(2):
                    for b in range(GROUP):
                        last = mm(ps[Q * b:Q * (b + 1), 1, 0:TOKENS], phat_kept[:, k, b, :], probs_t[:, b, k, :],
                                  k == 0, k == 1)
                last.then_inc(context_summed, 1)

            def turn_context(m):
                pe.wait_ge(context_rows_ready, m + 1)
                for h in range(2):
                    last = pe.transpose(ps[0:HALF, 1, 256 + 128 * h:256 + 128 * (h + 1)],
                                        context_rows[:, HALF * h:HALF * (h + 1)], ident)
                last.then_inc(context_ready, 1)

            def turn_u(m):
                pe.wait_ge(u_tok_ready, m + 1)
                pe.wait_ge(p_in_u_ready, m + 1)
                if not first(m):
                    pe.wait_ge(uhat_ready, m)
                for h in range(2):
                    last = pe.transpose(ps[:, 2, HALF * h:HALF * (h + 1)],
                                        u_tok[:, h].rearrange("p b r -> p (b r)"), ident[0:HALF, 0:HALF])
                last.then_inc(u_turned, 1)

            def apply_g2(m):
                pe.wait_ge(u_rows_ready, m + 1)
                for h in range(2):
                    last = mm(ps[0:HALF, 1, 128 * h:128 * (h + 1)], u_rows[:, HALF * h:HALF * (h + 1)], g2[:])
                last.then_inc(g2_summed, 1)

            def turn_uhat(m):
                pe.wait_ge(uhat_tok_ready, 2 * m + 2)
                for b in range(GROUP):
                    for h in range(2):
                        at = TOKENS * (b % 2) + HALF * h
                        last = pe.transpose(ps[:, 2 + b // 2, at:at + HALF],
                                            uhat_tok[:, h, b].rearrange("p c r -> p (c r)"),
                                            ident[0:HALF, 0:HALF])
                last.then_inc(uhat_turned, 1)

            def hidden(f, unit):
                if unit == 0:
                    pe.wait_ge(uhat_ready, f + 1)
                if not (first(f) and unit < 2):
                    pe.wait_ge(gelu_done, 12 * f + unit - 1)
                half, t = divmod(unit, HT)
                mm(ps[:, HB + unit % 2, 0:PAIR_TOKENS], f_stack[:, 128 * t:128 * (t + 1)],
                   uhat_stack[:, PAIR_TOKENS * half:PAIR_TOKENS * (half + 1)]).then_inc(hidden_summed, 1)

            def project(f, half, part):
                for r in range(4 * part, 4 * part + 4):
                    tile, t = divmod(r, HT)
                    b, h = 2 * half + tile // 2, tile % 2
                    o = ps[0:HALF, OB + tile % 2, 0:EMBED]
                    if t == 0:
                        if not (first(f) and half == 0 and tile < 2):
                            pe.wait_ge(out_ready, 8 * f + 4 * half + tile - 1)
                        pe.wait_ge(u_kept_ready[half], f + 1)
                        mm(o, u_kept[half][Q * b:Q * (b + 1), HALF * h:HALF * (h + 1)], resid[Q * b:Q * (b + 1), :],
                           True, False)
                    if tile == 0:
                        pe.wait_ge(h_lo_ready, 12 * f + HT * half + t + 1)
                    at = slice(HALF * tile, HALF * (tile + 1))
                    mm(o, h_hi[:, half, t, at], w1_hi[:, t, :], False, False)
                    mm(o, h_hi[:, half, t, at], w1_lo[:, t, :], False, False)
                    last = mm(o, h_lo[:, half, t, at], w1_hi[:, t, :], False, t == HT - 1)
                    if t == HT - 1:
                        last.then_inc(out_summed, 1)

            UNITS4 = {0: (2, 3), 1: (4, 5), 2: (6, 7), 3: (8, 9), 4: (10,), 7: (11,)}
            UNITS3 = {11: (0, 1)}
            PARTS5 = {0: [(1, 2)], 1: [(1, 3)], 2: [(1, 4), (1, 5)]}
            PARTS4 = {4: [(0, 0)], 5: [(0, 1)], 6: [(0, 2), (0, 3)], 7: [(0, 4)], 8: [(0, 5)], 10: [(1, 0)],
                      11: [(1, 1)]}

            def iteration(n, on):
                for slot in range(SLOTS):
                    if slot == 0 and 1 in on:
                        sum_rows(n - 1, 1)
                    if slot == 0 and 3 in on:
                        turn_u(n - 3)
                    if slot == 1 and 3 in on:
                        apply_g2(n - 3)
                    if slot == 3 and 2 in on:
                        scores(n - 2)
                    if slot == 7 and 2 in on:
                        turn_probs(n - 2)
                    if slot == 9 and 2 in on:
                        pe.wait_ge(probs_t_ready, 4 * (n - 2) + 4)
                    if slot == 9 and 1 in on:
                        turn_phat(n - 1)
                    if slot == 9 and 3 in on:
                        turn_uhat(n - 3)
                    if slot == 9 and 2 in on:
                        weigh(n - 2)
                    if slot == 10 and 1 in on:
                        apply_a(n - 1)
                    if slot == 10 and 2 in on:
                        turn_context(n - 2)
                    if 5 in on:
                        for half, part in PARTS5.get(slot, ()):
                            project(n - 5, half, part)
                    if 4 in on:
                        for half, part in PARTS4.get(slot, ()):
                            project(n - 4, half, part)
                        for unit in UNITS4.get(slot, ()):
                            hidden(n - 4, unit)
                    if slot == 11 and 0 in on:
                        sum_rows(n, 0)
                    if 3 in on:
                        for unit in UNITS3.get(slot, ()):
                            hidden(n - 3, unit)

            setup()
            pe.wait_ge(setup_dve, 14)
            pe.wait_ge(setup_act, ACT_W1)
            pe.wait_ge(setup_pool, 4)
            run(pe, iteration)

        @block.scalar
        def _(act):
            def setup():
                act.wait_ge(setup_pe, PE_CWT)
                act.copy(cwt[:], ps[0:E2, 0, 0:256].rearrange("p (k c) -> p k c", k=2))
                act.copy(cwt_48[:], ps[0:E2, 2, 0:2 * COLS].rearrange("p (k c) -> p k c", k=2))
                act.copy(cwt_ctx[:], ps[0:E2, 0, 256:512].rearrange("p (k c) -> p k c", k=2)).then_inc(setup_act, 1)
                act.wait_ge(setup_pe, PE_QKT)
                act.copy(qkt[:], ps[0:E2, 1, :].rearrange("p (j c) -> p j c", j=4)).then_inc(setup_act, 1)
                act.wait_ge(setup_pe, PE_COEF)
                act.copy(coef[:, :, 0:384], ps[0:E2, 2:4, 0:384])
                act.copy(coef[:, :, 384:768], ps[0:E2, 6:8, 0:384]).then_inc(setup_act, 1)
                act.wait_ge(setup_pe, PE_W0T)
                act.copy(w0t[:, :, 0:512], ps[0:E2, 2:4, :]).then_inc(setup_act, 1)
                act.copy(w0t[:, :, 512:768],
                         ps[0:E2, 7, :].rearrange("p (k c) -> p k c", k=2)).then_inc(setup_act, 1)
                act.wait_ge(setup_pe, PE_BASIS)
                act.copy(sel_gram[:, :, 1, :],
                         ps[:, 1, 0:TILES * IMAGE_PAIR].rearrange("p (t c) -> p t c", t=TILES))
                act.wait_ge(setup_pe, PE_BT)
                act.copy(basis_t[:], ps[0:E2, 2, 0:256].rearrange("p (k c) -> p k c", k=2)).then_inc(setup_act, 1)
                act.wait_ge(setup_pe, PE_F)
                act.copy(f_hi.rearrange("p (k c) -> p k c", k=2), ps[:, 4:6, 0:384]).then_inc(setup_act, 1)
                act.wait_ge(setup_pe, PE_W1)
                act.copy(w1_f32[:, 0:2, :], ps[:, 1, 0:384].rearrange("p (t e) -> p t e", t=2))
                act.copy(w1_f32[:, 2:6, :].rearrange("p (a t) e -> p a (t e)", a=2), ps[:, 6:8, 0:384])
                act.copy(w1_hi[:, 0:2, :], ps[:, 1, 0:384].rearrange("p (t e) -> p t e", t=2))
                act.copy(w1_hi[:, 2:6, :].rearrange("p (a t) e -> p a (t e)", a=2),
                         ps[:, 6:8, 0:384]).then_inc(setup_act, 1)

            def copy_p_tok(m):
                act.wait_ge(pool_summed, 2 * m + 2)
                if not first(m):
                    act.wait_ge(p_kept_ready, m)
                sums = ps[0:HALF, 0, 0:4 * COLS].rearrange("p (h g c) -> p h g c", h=2, g=2)
                act.copy(p_tok[:].rearrange("p h b r -> p h (b r)"), sums[:, :, 0, :]).then_inc(p_tok_ready, 1)

            def copy_phat(m):
                act.wait_ge(phat_turned, m + 1)
                act.copy(phat_rows[:], ps[:, 0, 0:TOKENS]).then_inc(phat_rows_ready, 1)

            def copy_b(m):
                act.wait_ge(b_summed, m + 1)
                act.copy(b_rows[:], ps[:, 0, 0:TOKENS]).then_inc(b_rows_ready, 1)

            def exponentials(m, images):
                for b in images:
                    act.wait_ge(max_ready, 4 * m + b + 1)
                    for h in range(2):
                        last = act.activation(probs[:, b, h, :], ps[0:HALF, b, TOKENS * h:TOKENS * (h + 1)], ACT.Exp,
                                              bias=neg_max[:, b, h:h + 1])
                    last.then_inc(probs_ready, 1)

            def copy_probs(m):
                for b in range(GROUP):
                    act.wait_ge(probs_turned, 4 * m + b + 1)
                    act.copy(probs_t[:, b].rearrange("p k q -> p (k q)"),
                             ps[0:HALF, b, 0:PAIR_TOKENS]).then_inc(probs_t_ready, 1)

            def copy_context(m):
                act.wait_ge(context_summed, m + 1)
                act.copy(context_rows[:], ps[:, 1, 0:TOKENS]).then_inc(context_rows_ready, 1)

            def copy_u(m):
                act.wait_ge(u_turned, m + 1)
                if not first(m):
                    act.wait_ge(u_kept_ready[0], m)
                act.copy(u_rows[:], ps[:, 2, 0:TOKENS]).then_inc(u_rows_ready, 1)

            def copy_uhat(m):
                act.wait_ge(uhat_turned, m + 1)
                act.copy(uhat_hi[:].rearrange("p (k c) -> p k c", k=2),
                         ps[:, 2:4, 0:PAIR_TOKENS]).then_inc(uhat_hi_ready, 1)

            def gelu(f, unit):
                half, t = divmod(unit, HT)
                act.wait_ge(hidden_summed, 12 * f + unit + 1)
                if not (first(f) and unit < 4):
                    act.wait_ge(h_lo_ready, 12 * f + unit - 3)
                if t == 0 and not first(f):
                    act.wait_ge(out_summed, 8 * f - 4 + 4 * half)
                summed = ps[:, HB + unit % 2, 0:PAIR_TOKENS]
                act.activation(h_f32[:, unit % 4, :], summed, ACT.Gelu_apprx_tanh)
                act.activation(h_hi[:, half, t, :], summed, ACT.Gelu_apprx_tanh).then_inc(gelu_done, 1)

            def take_out(f, half, tile):
                act.wait_ge(out_summed, 8 * f + 4 * half + tile + 1)
                if tile == 0 and not first(f):
                    act.wait_ge(out_sent[half], 16 * f)
                act.copy(out_sb[0:HALF, half, tile, :], ps[0:HALF, OB + tile % 2, 0:EMBED]).then_inc(out_ready, 1)

            UNITS4 = {0: (0, 1), 1: (2, 3), 2: (4, 5), 3: (6, 7), 4: (8, 9), 7: (10,), 8: (11,)}
            TAKES5 = {0: [(1, 0)], 1: [(1, 1)], 3: [(1, 2), (1, 3)]}
            TAKES4 = {6: [(0, 0)], 7: [(0, 1)], 8: [(0, 2)], 9: [(0, 3)]}

            def iteration(n, on):
                for slot in range(SLOTS):
                    if 5 in on:
                        for half, tile in TAKES5.get(slot, ()):
                            take_out(n - 5, half, tile)
                    if slot == 1 and 1 in on:
                        copy_p_tok(n - 1)
                    if slot == 5 and 2 in on:
                        exponentials(n - 2, (0, 1))
                    if 4 in on:
                        for half, tile in TAKES4.get(slot, ()):
                            take_out(n - 4, half, tile)
                    if slot == 6 and 2 in on:
                        exponentials(n - 2, (2, 3))
                    if slot == 8 and 2 in on:
                        copy_probs(n - 2)
                    if 4 in on:
                        for unit in UNITS4.get(slot, ()):
                            gelu(n - 4, unit)
                    if slot == 0 and 3 in on:
                        copy_u(n - 3)
                    if slot == 9 and 1 in on:
                        copy_phat(n - 1)
                    if slot == 9 and 3 in on:
                        copy_uhat(n - 3)
                    if slot == 10 and 2 in on:
                        copy_context(n - 2)
                    if slot == 10 and 1 in on:
                        copy_b(n - 1)

            setup()
            run(act, iteration, 1)

        @block.gpsimd
        def _(pool):
            def setup():
                pool.memset(stat[:], 1.0).then_inc(setup_pool_self, 1)
                pool.memset(phat_tok[:], 0.0).then_inc(setup_pool_self, 1)
                pool.memset(phat_kept[:], 0.0).then_inc(setup_pool_self, 1)
                pool.memset(u_tok[:], 0.0).then_inc(setup_pool_self, 1)
                pool.memset(uhat_tok[:], 0.0).then_inc(setup_pool_self, 1)
                pool.wait_ge(setup_pool_self, 5)
                pool.memset(phat_tok[:, :, :, ONE_P:ONE_P + 1], 1.0).then_inc(setup_pool_self, 1)
                pool.memset(phat_kept[:, :, :, ONE_P:ONE_P + 1], 1.0).then_inc(setup_pool_self, 1)
                pool.memset(u_tok[:, :, :, ONE_U:ONE_U + 1], 1.0).then_inc(setup_pool_self, 1)
                pool.memset(uhat_tok[:, :, :, :, ONE_F:ONE_F + 1].rearrange("p h b c r -> p (h b) c r"), 1.0).then_inc(setup_pool_self, 1)
                pool.wait_ge(setup_act, ACT_W0T)
                pool.tensor_tensor(w0t, w0t, coef, ALU.mult).then_inc(setup_pool, 1)
                pool.wait_ge(wproj_landed, 32)
                pool.tensor_tensor(wproj_sb[:], wproj_sb[:], coef, ALU.mult).then_inc(setup_pool, 1)
                pool.wait_ge(setup_act, ACT_W1)
                pool.tensor_tensor(w1_lo[:], w1_f32, w1_hi[:].bitcast(F32), ALU.subtract).then_inc(setup_pool, 1)
                pool.memset(zero[:], 0.0).then_inc(setup_pool_self, 1)
                pool.memset(three_halves[:], 1.5).then_inc(setup_pool, 1)
                pool.wait_ge(setup_pool, 4)
                pool.wait_ge(setup_pool_self, 10)

            inv_std = stat[:, 2].rearrange("p k (h b) -> p k h b", h=2)

            def inverse_roots(n):
                at = 12 * (n - 1)
                pool.wait_ge(stat_steps, 4 * n)
                h, y = stat[:, 3], stat[:, 2]
                for step in range(3):
                    pool.tensor_tensor(newton[:], y, y, ALU.mult).then_inc(newton_steps, 1)
                    pool.wait_ge(newton_steps, at + 4 * step + 1)
                    pool.tensor_tensor(newton[:], newton[:], h, ALU.mult).then_inc(newton_steps, 1)
                    pool.wait_ge(newton_steps, at + 4 * step + 2)
                    pool.tensor_tensor(newton[:], newton[:], three_halves[:], ALU.add).then_inc(newton_steps, 1)
                    pool.wait_ge(newton_steps, at + 4 * step + 3)
                    pool.tensor_tensor(y, y, newton[:], ALU.mult).then_inc(newton_steps, 1)
                    pool.wait_ge(newton_steps, at + 4 * step + 4)

            def scale_p(m):
                if not first(m):
                    pool.wait_ge(phat_kept_ready, m)
                for h in range(2):
                    pool.tensor_tensor(phat_tok[:, h, :, 0:CHANNELS], p_tok[:, h],
                                       inv_std[:, 0, h, :].unsqueeze(2).broadcast_to([HALF, GROUP, CHANNELS]),
                                       ALU.mult).then_inc(phat_tok_ready, 1)

            def scale_u():
                shape = [HALF, GROUP, 4, BASIS]
                for h in range(2):
                    pool.tensor_tensor(uhat_tok[:, h, :, :, 0:BASIS],
                                       u_tok[:, h, :, 0:BASIS].unsqueeze(2).broadcast_to(shape),
                                       inv_std[:, 1, h, :].unsqueeze(2).unsqueeze(3).broadcast_to(shape),
                                       ALU.mult).then_inc(uhat_tok_ready, 1)

            def low_part(f, unit):
                half, t = divmod(unit, HT)
                pool.wait_ge(gelu_done, 12 * f + unit + 1)
                pool.tensor_tensor(h_lo[:, half, t, :], h_f32[:, unit % 4, :], h_hi[:, half, t, :].bitcast(F32),
                                   ALU.subtract).then_inc(h_lo_ready, 1)

            def p_columns(a):
                return a[:, :, :, 0:CHANNELS].rearrange("p h b r -> p (h b) r")

            zeros = zero[0:HALF, :].unsqueeze(2).broadcast_to([HALF, 2 * GROUP, CHANNELS])

            def p_into_u(m):
                pool.wait_ge(p_kept_ready, m + 1)
                if not first(m):
                    pool.wait_ge(uhat_tok_ready, 2 * m)
                pool.tensor_tensor(p_columns(u_tok), p_columns(p_kept), zeros, ALU.add).then_inc(p_in_u_ready, 1)

            def keep_p(m):
                pool.wait_ge(p_tok_ready, m + 1)
                if not first(m):
                    pool.wait_ge(p_in_u_ready, m)
                pool.tensor_tensor(p_columns(p_kept), p_columns(p_tok), zeros, ALU.add).then_inc(p_kept_ready, 1)

            def keep_phat(m):
                pool.wait_ge(phat_tok_ready, 2 * m + 2)
                if not first(m):
                    pool.wait_ge(context_summed, m)
                pool.tensor_tensor(p_columns(phat_kept), p_columns(phat_tok), zeros,
                                   ALU.add).then_inc(phat_kept_ready, 1)

            def keep_u(f, half):
                if half == 0:
                    pool.wait_ge(u_rows_ready, f + 1)
                else:
                    pool.wait_ge(u_kept_ready[0], f + 1)
                if not first(f):
                    pool.wait_ge(out_summed, 8 * f - 4 + 4 * half)
                    if half == 0:
                        pool.wait_ge(u_kept_ready[1], f)
                pool.tensor_tensor(u_kept[half][:], (u_rows, u_kept[0])[half][:],
                                   zero[:].broadcast_to([128, TOKENS]), ALU.add).then_inc(u_kept_ready[half], 1)

            def iteration(n, on):
                if 4 in on:
                    for unit in range(HT):
                        low_part(n - 4, unit)
                if 1 in on or 3 in on:
                    inverse_roots(n)
                if 1 in on:
                    scale_p(n - 1)
                if 3 in on:
                    scale_u()
                if 4 in on:
                    for unit in range(HT, 10):
                        low_part(n - 4, unit)
                    keep_u(n - 4, 1)
                if 2 in on:
                    p_into_u(n - 2)
                if 1 in on:
                    keep_p(n - 1)
                if 4 in on:
                    for unit in range(10, 12):
                        low_part(n - 4, unit)
                if 3 in on:
                    keep_u(n - 3, 0)
                if 1 in on:
                    keep_phat(n - 1)

            setup()
            run(pool, iteration, 1)


def kernel(x, L0_tok_channel_weights, L0_attn_W_qkv, L0_attn_b_qkv, L0_ffn_w_fc, L0_ffn_b_fc, L0_ffn_w_proj,
           L0_ffn_b_proj, L0_ffn_alpha_e, L0_ffn_alpha_r):
    import concourse.bacc as bacc
    from concourse.bass_utils import run_bass_kernel_spmd

    full, rows, paired = constants()
    arrays = {
        "x": x, "cw": L0_tok_channel_weights, "wqkv": L0_attn_W_qkv, "bqkv": L0_attn_b_qkv.reshape(1, -1),
        "wfc": L0_ffn_w_fc, "bfc": L0_ffn_b_fc.reshape(1, -1), "wproj": L0_ffn_w_proj,
        "bproj": L0_ffn_b_proj.reshape(1, -1),
        "alpha_e": np.repeat(L0_ffn_alpha_e, len(RATIO_CHOICES)).reshape(-1, 1),
        "alpha_r": np.tile(L0_ffn_alpha_r, len(EMBED_CHOICES)).reshape(-1, 1),
        "const_full": full, "const_rows": rows, "const_paired": paired,
    }
    arrays = {k: np.ascontiguousarray(v) for k, v in arrays.items()}
    nc = bacc.Bacc("TRN2", target_bir_lowering=False, num_devices=1)
    args = [nc.dram_tensor(k, v.shape, F32, kind="ExternalInput").ap() for k, v in arrays.items()]
    out = nc.dram_tensor("out", (IMAGES, TOKENS, EMBED), F32, kind="ExternalOutput").ap()
    build(nc, *args, out)
    r = run_bass_kernel_spmd(nc, [arrays], core_ids=[0])
    return r.results[0]["out"]
```

```python
from contextlib import ExitStack

import numpy as np

import concourse.bass as bass
from concourse import mybir

F32 = mybir.dt.float32
F32R = mybir.dt.float32r
I32 = mybir.dt.int32
ALU = mybir.AluOpType
ACT = mybir.ActivationFunctionType
AX = mybir.AxisListType

IMAGES, CHANNELS, SIDE = 64, 12, 224
PATCH = 16
GRID = SIDE // PATCH
TOKENS = GRID * GRID
EMBED = 192
HIDDEN = 768
EPS = 1e-5
EMBED_CHOICES = (96, 144, 192)
RATIO_CHOICES = (2, 3, 4)
MIXES = len(EMBED_CHOICES) * len(RATIO_CHOICES)

GROUP = 4
GROUPS = IMAGES // GROUP
Q = 32
HALF = TOKENS // 2
PAIRS = 8
TILES = GROUP * CHANNELS // PAIRS
E2 = EMBED // 2
HT = HIDDEN // 128
PAIR_TOKENS = 2 * TOKENS

ONE_P = CHANNELS
CTX = CHANNELS
ONE_U = 2 * CHANNELS
BASIS = ONE_U + 1
ONE_F = BASIS

COLS = GROUP * CHANNELS
IMAGE_PAIR = 2 * CHANNELS
SEL_AT = 128
MASK_G = SEL_AT + TILES * IMAGE_PAIR
MASK_S, LO_ACT, LO_W = MASK_G + 128, MASK_G + 256, MASK_G + 257
QUADRANT = LO_W + 1
FULL = QUADRANT + GROUP
ROW_P, ROW_C, ROW_ONE_U, ROW_ONE_P, ROW_ONE_F, ROW_IN = 0, 128, 256, 384, 512, 640
ROW_OUT = ROW_IN + EMBED
ROW_48 = ROW_OUT + HIDDEN
ROWS = ROW_48 + COLS
PAIR_MASK = TILES * 128
PAIRED = PAIR_MASK + COLS

SLOTS = 12
STEPS = 4 * SLOTS
LAG = 3
MAGIC = float(0x5F3759DF)

PE_ORDER = {
    "loop": {
        "sum_rows": (31, 47), "turn_phat": 61, "apply_a": 63, "scores": 65, "turn_probs": 71, "weigh": 74,
        "turn_context": 78, "turn_u": 81, "apply_g2": 86, "turn_uhat": 116,
        "hidden": (123, 124, 130, 132, 134, 137, 140, 141, 143, 145, 148, 148),
        "project": (139, 142, 147, 148, 148, 152, 153, 154, 154, 156, 157, 159, 161, 163, 165, 166, 168, 169, 173,
            175, 177, 180, 182, 185),
    },
    0: {
        "hidden": (122, 123, 130, 136, 139, 141, 143, 143, 143, 145, 148, 148),
    },
    13: {
        "project": (139, 142, 146, 147, 151, 157, 157, 157, 157, 157, 157, 159, 161, 163, 165, 166, 168, 169, 173,
            175, 178, 182, 183, 183),
    },
    14: {
        "project": (138, 141, 146, 147, 150, 151, 152, 153, 154, 155, 156, 158, 165, 165, 165, 166, 168, 168, 172,
            174, 178, 180, 183, 183),
    },
    15: {
        "hidden": (122, 123, 129, 131, 134, 136, 136, 140, 142, 145, 148, 152),
        "project": (138, 141, 143, 147, 150, 151, 152, 153, 154, 155, 156, 156, 157, 159, 161, 162, 164, 165, 169,
            171, 175, 177, 181, 181),
    },
}
ACT_ORDER = {
    "loop": {
        "copy_p_tok": 48, "copy_phat": 60, "copy_b": 61, "exponentials": 65, "copy_probs": 69, "copy_context": 74,
        "copy_u": 79, "copy_uhat": 115, "gelu": (124, 124, 132, 133, 134, 141, 141, 141, 142, 146, 154, 156),
        "take_out": (147, 150, 155, 160, 167, 167, 182, 185),
    },
}
POOL_ORDER = {
    "loop": {
        "p_into_u": 65, "keep_u": (109, 143),
        "low_part": (123, 123, 123, 123, 124, 124, 124, 133, 136, 145, 157, 157),
    },
}
DVE_ORDER = {
    "loop": {
        "maxima": 17, "context": 19, "low_parts": 30,
    },
    0: {
        "low_parts": 31,
    },
    1: {
        "maxima": 18,
    },
}
PE_SETUP = {"basis": (0, 32), "gram": (1, 5), "f": (1, 23), "w1": (1, 38)}
ACT_SETUP = {"basis": (0, 41), "f": (1, 38), "w1": (1, 44)}
DVE_SETUP = {"centre": (0, 0), "gram": (0, 1), "scores": (0, 5), "biases": (0, 9), "basis": (1, 0),
             "g2": (1, 0), "f": (1, 8)}


def constants():
    full = np.zeros((128, FULL), np.float32)
    full[:, :128] = np.eye(128)
    for t in range(TILES):
        for p in range(128):
            b, c = divmod(PAIRS * t + p % PAIRS, CHANNELS)
            full[p, SEL_AT + IMAGE_PAIR * t + CHANNELS * (b % 2) + c] = 1.0
    block = np.kron(np.eye(GROUP), np.ones((Q, Q)))
    full[:, MASK_G:MASK_G + 128] = block / EMBED
    full[:, MASK_S:MASK_S + 128] = block / np.sqrt(EMBED)
    quadrant = np.arange(128) // Q
    full[:, LO_ACT] = -(quadrant % 2)
    full[:, LO_W] = -(quadrant // 2)
    full[:, QUADRANT:] = np.kron(np.eye(GROUP), np.ones((Q, 1)))
    rows = np.zeros((CHANNELS, ROWS), np.float32)
    for b in range(GROUP):
        for c in range(CHANNELS):
            rows[c, ROW_P + Q * b + c] = 1.0
            rows[c, ROW_C + Q * b + CTX + c] = 1.0
            rows[c, ROW_48 + CHANNELS * b + c] = 1.0
        rows[0, ROW_ONE_U + Q * b + ONE_U] = 1.0
        rows[0, ROW_ONE_P + Q * b + ONE_P] = 1.0
        rows[0, ROW_ONE_F + Q * b + ONE_F] = 1.0
    for i, e in enumerate(EMBED_CHOICES):
        for j, r in enumerate(RATIO_CHOICES):
            k = len(RATIO_CHOICES) * i + j
            rows[k, ROW_IN:ROW_IN + e] = 1.0
            rows[k, ROW_OUT:ROW_OUT + r * e] = 1.0
    paired = np.zeros((COLS, PAIRED), np.float32)
    for t in range(TILES):
        for p in range(128):
            paired[PAIRS * t + p % PAIRS, 128 * t + p] = 1.0
    paired[:, PAIR_MASK:] = np.kron(np.eye(GROUP), np.ones((CHANNELS, CHANNELS))) / EMBED
    return full, rows, paired


def build(nc, x, cw, wqkv, bqkv, wfc, bfc, wproj, bproj, alpha_e, alpha_r, const_full, const_rows, const_paired, out):
    with ExitStack() as ctx:
        def sb(name, shape, dt=F32):
            return ctx.enter_context(nc.sbuf_tensor(name, shape, dt))

        def sem(name):
            return ctx.enter_context(nc.semaphore(name))

        cf = sb("cf", [128, FULL])
        cr = sb("cr", [CHANNELS, ROWS])
        cw_sb = sb("cw_sb", [CHANNELS, EMBED])
        cw_mean = sb("cw_mean", [CHANNELS, 1])
        cwc = sb("cwc", [CHANNELS, EMBED])
        wqkv_sb = sb("wqkv_sb", [E2, 2, 3 * EMBED])
        bqkv_sb = sb("bqkv_sb", [1, 3 * EMBED])
        bfc_sb = sb("bfc_sb", [1, HIDDEN])
        wproj_sb = sb("wproj_sb", [E2, 2, HIDDEN])
        bproj_sb = sb("bproj_sb", [1, EMBED])
        alpha_sb = sb("alpha_sb", [MIXES, 2])
        mix = sb("mix", [MIXES, 1])
        mix_in = sb("mix_in", [MIXES, EMBED])
        cwt_ctx = sb("cwt_ctx", [E2, 2, 128])
        cwt_48 = sb("cwt_48", [E2, 2, COLS])
        gram_48 = sb("gram_48", [COLS, COLS])
        qkt = sb("qkt", [E2, 4, 128])
        basis_mean = sb("basis_mean", [128, 1])
        basis_t = sb("basis_t", [E2, 2, 128])
        sel_gram = sb("sel_gram", [128, TILES, 2, IMAGE_PAIR])
        score_mat = sb("score_mat", [128, 128])
        g2 = sb("g2", [128, 128])
        resid = sb("resid", [128, GROUP, EMBED])
        f_stack = sb("f_stack", [128, HIDDEN], F32R)
        w1_hi = sb("w1_hi", [128, HT, EMBED], F32R)
        w1_lo = sb("w1_lo", [128, HT, EMBED], F32R)
        xs = sb("xs", [128, TILES, GRID, SIDE])
        pooled = sb("pooled", [128, TILES, TOKENS])
        p_tok = sb("p_tok", [HALF, 2, GROUP, CHANNELS])
        context_rows = sb("context_rows", [128, TOKENS])
        u_tok = sb("u_tok", [HALF, 2, GROUP, Q])
        phat_tok = sb("phat_tok", [HALF, 2, GROUP, Q])
        uhat_tok = sb("uhat_tok", [HALF, 2, GROUP, 4, Q])
        prod = sb("prod", [HALF, 2, 2, GROUP, BASIS])
        stat = sb("stat", [HALF, 4, 2, 2 * GROUP])
        newton = sb("newton", [HALF, 2, 2 * GROUP])
        phat_rows = sb("phat_rows", [128, TOKENS])
        b_rows = sb("b_rows", [128, TOKENS])
        neg_max = sb("neg_max", [HALF, GROUP, 2])
        probs = sb("probs", [HALF, GROUP, 2, TOKENS])
        probs_t = sb("probs_t", [HALF, GROUP, 2, TOKENS])
        three_halves = sb("three_halves", [HALF, 2, 2 * GROUP])
        zero = sb("zero", [128, 1])
        row_inv = sb("row_inv", [HALF, 2, GROUP])
        u_rows = sb("u_rows", [128, TOKENS])
        u_kept = [sb("u_kept0", [128, TOKENS]), sb("u_kept1", [128, TOKENS])]
        uhat_hi = sb("uhat_hi", [128, GROUP * TOKENS], F32R)
        uhat_stack = sb("uhat_stack", [128, GROUP * TOKENS], F32R)
        h_f32 = sb("h_f32", [128, 4, PAIR_TOKENS])
        h_hi = sb("h_hi", [128, 2, HT, PAIR_TOKENS], F32R)
        h_lo = sb("h_lo", [128, 2, HT, PAIR_TOKENS], F32R)
        out_sb = sb("out_sb", [128, 2, GROUP, EMBED])
        coef = probs[0:E2].rearrange("p b h k -> p (b h k)")[:, 0:2 * HIDDEN].rearrange("p (k h) -> p k h", k=2)
        w0t = h_f32[0:E2].rearrange("p s c -> p (s c)")[:, 0:2 * HIDDEN].rearrange("p (k h) -> p k h", k=2)
        cwt = prod[0:E2].rearrange("p n h b r -> p (n h b r)")[:, 0:256].rearrange("p (k c) -> p k c", k=2)
        wfc_sb = out_sb[:].rearrange("p h b e -> p (h b) e")[:, 0:HT, :]
        paired_sb = h_f32[0:COLS].rearrange("p s c -> p (s c)")[:, 0:PAIRED]
        w1_f32 = h_f32[:].rearrange("p s c -> p (s c)")[:, 0:HT * EMBED].rearrange("p (t e) -> p t e", t=HT)
        basis_sb, basis_c = out_sb[:, 1, 2, :], out_sb[:, 1, 3, :]
        f_hi = uhat_hi[:, 0:HIDDEN]

        ps = ctx.enter_context(nc.psum_tensor("ps", [128, 8, 512], F32))
        HB, OB = 4, 6

        x_landed = [sem(f"x_landed{t}") for t in range(TILES)]
        cf_landed = sem("cf_landed")
        cr_landed = sem("cr_landed")
        cw_landed = sem("cw_landed")
        wqkv_landed = sem("wqkv_landed")
        mix_landed = sem("mix_landed")
        wfc_landed = sem("wfc_landed")
        wproj_landed = sem("wproj_landed")
        setup_pe = sem("setup_pe")
        setup_act = sem("setup_act")
        setup_dve = sem("setup_dve")
        setup_pool = sem("setup_pool")
        setup_pool_self = sem("setup_pool_self")
        reduced = sem("reduced")
        pool_summed = sem("pool_summed")
        p_tok_ready = sem("p_tok_ready")
        stat_steps = sem("stat_steps")
        newton_steps = sem("newton_steps")
        phat_tok_ready = sem("phat_tok_ready")
        phat_turned = sem("phat_turned")
        phat_rows_ready = sem("phat_rows_ready")
        b_summed = sem("b_summed")
        b_rows_ready = sem("b_rows_ready")
        scores_ready = sem("scores_ready")
        max_ready = sem("max_ready")
        probs_ready = sem("probs_ready")
        probs_turned = sem("probs_turned")
        probs_t_ready = sem("probs_t_ready")
        context_summed = sem("context_summed")
        context_rows_ready = sem("context_rows_ready")
        context_ready = sem("context_ready")
        p_in_u_ready = sem("p_in_u_ready")
        row_inv_ready = sem("row_inv_ready")
        u_tok_ready = sem("u_tok_ready")
        u_turned = sem("u_turned")
        u_rows_ready = sem("u_rows_ready")
        g2_summed = sem("g2_summed")
        uhat_tok_ready = sem("uhat_tok_ready")
        uhat_turned = sem("uhat_turned")
        uhat_hi_ready = sem("uhat_hi_ready")
        uhat_ready = sem("uhat_ready")
        u_kept_ready = [sem("u_kept0_ready"), sem("u_kept1_ready")]
        hidden_summed = sem("hidden_summed")
        gelu_done = sem("gelu_done")
        h_lo_ready = sem("h_lo_ready")
        out_summed = sem("out_summed")
        out_ready = sem("out_ready")
        out_sent = [sem("out_sent0"), sem("out_sent1")]

        ident = cf[:, 0:128]
        x_tiles = x.rearrange("(n b) c (i k) w -> n k (b c) i w", b=GROUP, k=PATCH)
        out_tiles = out.rearrange("(n b) (h p) e -> n p b h e", b=2, h=2)

        PE_CWT, PE_G1, PE_ROWS, PE_QKT, PE_A, PE_COEF, PE_W0T, PE_BASIS, PE_BT, PE_G2, PE_F, PE_W1 = range(1, 13)
        ACT_CWT, ACT_SEL, ACT_QKT, ACT_COEF, ACT_W0T, ACT_BT, ACT_FHI, ACT_W1 = range(1, 9)
        DVE_CWC, DVE_MIX, DVE_GRAM, DVE_SCORE, DVE_BIAS, DVE_BASIS, DVE_CENTRED, DVE_G2, DVE_F = (
            3, 5, 6, 7, 8, 9, 12, 13, 14)
        POOL_W0T, POOL_WPROJ, POOL_W1 = range(1, 4)

        block = ctx.enter_context(nc.Block())

        def first(n):
            return is_step(n, 0)

        def order(table, m):
            return {**table["loop"], **table.get(m, {})} if isinstance(m, int) else table["loop"]

        def is_step(n, k):
            return isinstance(n, int) and n == k

        def run(engine, iteration, start=0):
            for n in range(start, GROUPS + LAG):
                if n == LAG:
                    with engine.Fori(LAG, GROUPS) as i:
                        iteration(i, set(range(LAG + 1)))
                elif n < LAG or n >= GROUPS:
                    iteration(n, {k for k in range(LAG + 1) if 0 <= n - k < GROUPS})

        @block.sync
        def _(sp):
            def load(n, t):
                sp.dma_start(xs[:, t], x_tiles[n, :, PAIRS * t:PAIRS * (t + 1)]).then_inc(x_landed[t], 16)

            def reload(n, t):
                sp.wait_ge(reduced, SLOTS * (n - 1) + 2 * t + 2)
                load(n, t)

            def send(m, half):
                sp.wait_ge(out_ready, 8 * m + 4 * half + 4)
                sp.dma_start(out_tiles[2 * m + half],
                             out_sb[0:HALF, half].rearrange("p (b h) e -> p b h e", b=2)).then_inc(out_sent[half], 16)

            def iteration(n, on, loads=True):
                for t in range(TILES):
                    if loads:
                        reload(n + 1, t)
                    if t == 1 and 3 in on:
                        send(n - 3, 0)
                    if t == 4 and 3 in on:
                        send(n - 3, 1)

            load(0, 0)
            sp.dma_start(cr[:], const_rows).then_inc(cr_landed, 16)
            sp.dma_start(cw_sb[:], cw).then_inc(cw_landed, 16)
            sp.dma_start(cf[:], const_full).then_inc(cf_landed, 16)
            sp.dma_start(paired_sb, const_paired).then_inc(cf_landed, 16)
            sp.dma_start(alpha_sb[:, 0:1], alpha_e).then_inc(mix_landed, 16)
            sp.dma_start(alpha_sb[:, 1:2], alpha_r).then_inc(mix_landed, 16)
            sp.dma_start(bqkv_sb[:], bqkv).then_inc(wqkv_landed, 16)
            sp.dma_start(wqkv_sb[:], wqkv.rearrange("(k p) n -> p k n", k=2)).then_inc(wqkv_landed, 16)
            load(0, 1)
            load(0, 2)
            sp.dma_start(bfc_sb[:], bfc).then_inc(wfc_landed, 16)
            sp.dma_start(wfc_sb, wfc.rearrange("(t p) e -> p t e", p=128)).then_inc(wfc_landed, 16)
            load(0, 3)
            sp.dma_start(bproj_sb[:], bproj).then_inc(wproj_landed, 16)
            sp.dma_start(wproj_sb[:], wproj.rearrange("(k p) h -> p k h", k=2)).then_inc(wproj_landed, 16)
            load(0, 4)
            load(0, 5)
            for n in range(LAG):
                iteration(n, set(range(n + 1)))
            with sp.Fori(LAG, GROUPS - 1) as n:
                iteration(n, set(range(LAG + 1)))
            for n in range(GROUPS - 1, GROUPS + LAG):
                iteration(n, {k for k in range(LAG + 1) if n - k < GROUPS}, loads=False)
            for half in range(2):
                sp.wait_ge(out_sent[half], 16 * GROUPS)

        @block.vector
        def _(dve):
            def reduce_half(n, slot):
                t, half = divmod(slot, 2)
                if half == 0:
                    dve.wait_ge(x_landed[t], 16 * n + 16)
                    if not first(n):
                        dve.wait_ge(pool_summed, 2 * n - 1 if t < TILES // 2 else 2 * n)
                rows = xs[:, t, 7 * half:7 * half + 7, :].rearrange("p i (j k) -> p (i j) k", k=PATCH)
                dve.tensor_reduce(pooled[:, t, HALF * half:HALF * (half + 1)], rows, AX.X,
                                  ALU.add).then_inc(reduced, 1)

            def statistics(n, norm1, norm2):
                at = 4 * (n - 1)
                if is_step(n, 1):
                    dve.wait_ge(setup_pool_self, 9)
                if norm1:
                    dve.wait_ge(p_tok_ready, n)
                    gram = ps[0:HALF, 0, 0:4 * COLS].rearrange("p (h g b r) -> p h g b r", h=2, g=2, b=GROUP)
                    for h in range(2):
                        last = dve.tensor_tensor(prod[:, 0, h, :, 0:CHANNELS], p_tok[:, h], gram[:, h, 1], ALU.mult)
                if norm2:
                    dve.wait_ge(g2_summed, n - 1)
                    gram2 = ps[0:HALF, 1, 0:256].rearrange("p (h b r) -> p h b r", h=2, b=GROUP)
                    for h in range(2):
                        last = dve.tensor_tensor(prod[:, 1, h], u_tok[:, h, :, 0:BASIS], gram2[:, h, :, 0:BASIS],
                                                 ALU.mult)
                last.then_inc(stat_steps, 1)
                dve.wait_ge(stat_steps, at + 1)
                if norm1:
                    last = dve.tensor_reduce(stat[:, 0, 0, :],
                                             prod[:, 0, :, :, 0:CHANNELS].rearrange("p h b r -> p (h b) r"),
                                             AX.X, ALU.add)
                if norm2:
                    last = dve.tensor_reduce(stat[:, 0, 1, :], prod[:, 1].rearrange("p h b r -> p (h b) r"),
                                             AX.X, ALU.add)
                last.then_inc(stat_steps, 1)
                dve.wait_ge(stat_steps, at + 2)
                dve.tensor_scalar(stat[:, 1], stat[:, 0], EPS, None, ALU.add).then_inc(stat_steps, 1)
                dve.wait_ge(stat_steps, at + 3)
                dve.tensor_scalar(stat[:, 3], stat[:, 1], -0.5, None, ALU.mult)
                dve.tensor_scalar(stat[:, 2].bitcast(I32), stat[:, 1].bitcast(I32), -0.5, MAGIC,
                                  ALU.mult, ALU.add).then_inc(stat_steps, 1)

            def maxima(m):
                for b in range(GROUP):
                    dve.wait_ge(scores_ready, 4 * m + b + 1)
                    dve.tensor_reduce(neg_max[:, b, :],
                                      ps[0:HALF, b, 0:PAIR_TOKENS].rearrange("p (h k) -> p h k", h=2),
                                      AX.X, ALU.max, negate=True).then_inc(max_ready, 1)

            def context(m):
                dve.wait_ge(context_ready, m + 1)
                sums = ps[0:HALF, 1, 256:512].rearrange("p (h b r) -> p h b r", h=2, b=GROUP)
                dve.reciprocal(row_inv[:], sums[:, :, :, ONE_P]).then_inc(row_inv_ready, 1)
                dve.wait_ge(row_inv_ready, m + 1)
                for h in range(2):
                    last = dve.tensor_tensor(u_tok[:, h, :, CTX:ONE_U], sums[:, h, :, 0:CHANNELS],
                                             row_inv[:, h, :].unsqueeze(2).broadcast_to([HALF, GROUP, CHANNELS]),
                                             ALU.mult)
                last.then_inc(u_tok_ready, 1)

            def low_parts(f):
                dve.wait_ge(uhat_hi_ready, f + 1)
                if not first(f):
                    dve.wait_ge(hidden_summed, 12 * f)
                for k in range(2):
                    last = dve.scalar_tensor_tensor(
                        out=uhat_stack[:, PAIR_TOKENS * k:PAIR_TOKENS * (k + 1)],
                        in0=uhat_hi[:, PAIR_TOKENS * k:PAIR_TOKENS * (k + 1)].bitcast(F32),
                        scalar=cf[:, LO_ACT:LO_ACT + 1], in1=ps[:, HB + k, 0:PAIR_TOKENS],
                        op0=ALU.mult, op1=ALU.add)
                last.then_inc(uhat_ready, 1)

            def setup_centre():
                dve.wait_ge(cw_landed, 16)
                dve.tensor_reduce(cw_mean[:], cw_sb[:], AX.X, ALU.add, negate=True).then_inc(setup_dve, 1)
                dve.wait_ge(setup_dve, 1)
                dve.tensor_scalar(cw_mean[:], cw_mean[:], 1.0 / EMBED, None, ALU.mult).then_inc(setup_dve, 1)
                dve.wait_ge(setup_dve, 2)
                dve.tensor_scalar(cwc[:], cw_sb[:], cw_mean[:], None, ALU.add).then_inc(setup_dve, 1)
                dve.wait_ge(mix_landed, 32)
                dve.tensor_tensor(mix[:], alpha_sb[:, 0:1], alpha_sb[:, 1:2], ALU.mult).then_inc(setup_dve, 1)
                dve.wait_ge(setup_dve, 4)
                dve.wait_ge(cr_landed, 16)
                dve.tensor_scalar(mix_in[:], cr[0:MIXES, ROW_IN:ROW_IN + EMBED], mix[:], None,
                                  ALU.mult).then_inc(setup_dve, 1)

            def setup_gram():
                dve.wait_ge(cf_landed, 32)
                dve.tensor_copy(sel_gram[:, :, 0, :], cf[:, SEL_AT:MASK_G].rearrange("p (t c) -> p t c", t=TILES))
                dve.wait_ge(setup_pe, PE_G1)
                dve.tensor_tensor(gram_48[:], ps[0:COLS, 0, 0:COLS], paired_sb[:, PAIR_MASK:],
                                  ALU.mult).then_inc(setup_dve, 1)

            def setup_scores():
                dve.wait_ge(setup_pe, PE_A)
                dve.tensor_tensor(score_mat[:], ps[:, 1, 0:128], cf[:, MASK_S:MASK_S + 128],
                                  ALU.mult).then_inc(setup_dve, 1)

            def setup_biases():
                dve.wait_ge(setup_pe, PE_W0T)
                dve.wait_ge(wfc_landed, 32)
                dve.wait_ge(wproj_landed, 32)
                for k in range(2):
                    dve.tensor_tensor(bfc_sb[0:1, 384 * k:384 * (k + 1)], bfc_sb[0:1, 384 * k:384 * (k + 1)],
                                      ps[0:1, 4 + k, 0:384], ALU.mult)
                dve.tensor_tensor(bproj_sb[:], bproj_sb[:], ps[0:1, 6, 0:EMBED], ALU.mult).then_inc(setup_dve, 1)

            def setup_basis():
                dve.wait_ge(setup_pe, PE_BASIS)
                for b in range(GROUP):
                    dve.tensor_scalar(resid[:, b], ps[:, 3, 256:256 + EMBED], cf[:, QUADRANT + b:QUADRANT + b + 1],
                                      None, ALU.mult)
                dve.tensor_copy(basis_sb, ps[:, 3, 0:EMBED]).then_inc(setup_dve, 1)
                dve.wait_ge(setup_dve, DVE_BASIS)
                dve.tensor_reduce(basis_mean[:], basis_sb, AX.X, ALU.add, negate=True).then_inc(setup_dve, 1)
                dve.wait_ge(setup_dve, 10)
                dve.tensor_scalar(basis_mean[:], basis_mean[:], 1.0 / EMBED, None, ALU.mult).then_inc(setup_dve, 1)
                dve.wait_ge(setup_dve, 11)
                dve.tensor_scalar(basis_c, basis_sb, basis_mean[:], None, ALU.add).then_inc(setup_dve, 1)

            def setup_g2():
                dve.wait_ge(setup_pe, PE_G2)
                dve.tensor_tensor(g2[:], ps[:, 1, 0:128], cf[:, MASK_G:MASK_G + 128], ALU.mult).then_inc(setup_dve, 1)

            def setup_f():
                dve.wait_ge(setup_act, ACT_FHI)
                for k in range(2):
                    last = dve.scalar_tensor_tensor(
                        out=f_stack[:, 384 * k:384 * (k + 1)], in0=f_hi[:, 384 * k:384 * (k + 1)].bitcast(F32),
                        scalar=cf[:, LO_W:LO_W + 1], in1=ps[:, 4 + k, 0:384], op0=ALU.mult, op1=ALU.add)
                last.then_inc(setup_dve, 1)

            SETUP = {"centre": setup_centre, "gram": setup_gram, "scores": setup_scores, "biases": setup_biases,
                     "basis": setup_basis, "g2": setup_g2, "f": setup_f}

            def iteration(n, on):
                for slot in range(SLOTS):
                    if 0 in on:
                        reduce_half(n, slot)
                    for piece, build_piece in SETUP.items():
                        if is_step(n, DVE_SETUP[piece][0]) and slot == DVE_SETUP[piece][1]:
                            build_piece()
                    if slot == 0 and (1 in on or 2 in on):
                        statistics(n, 1 in on, 2 in on)
                    for k in sorted(on, reverse=True):
                        m, now = n - k, SLOTS * k + slot
                        at = order(DVE_ORDER, m)
                        if now == at["maxima"]:
                            maxima(m)
                        if now == at["context"]:
                            context(m)
                        if now == at["low_parts"]:
                            low_parts(m)

            run(dve, iteration)

        @block.tensor
        def _(pe):
            def mm(o, a, b, start=True, stop=True):
                return pe.matmul(o, a, b, start=start, stop=stop)

            def setup():
                pe.wait_ge(cr_landed, 16)
                pe.wait_ge(setup_dve, DVE_CWC)
                for k in range(2):
                    mm(ps[0:E2, 2, COLS * k:COLS * (k + 1)], cwc[:, E2 * k:E2 * (k + 1)],
                       cr[:, ROW_48:ROW_48 + COLS])
                for at, row in ((0, ROW_P), (256, ROW_C)):
                    for k in range(2):
                        last = mm(ps[0:E2, 0, at + 128 * k:at + 128 * (k + 1)], cwc[:, E2 * k:E2 * (k + 1)],
                                  cr[:, row:row + 128])
                last.then_inc(setup_pe, 1)
                pe.wait_ge(setup_act, ACT_CWT)
                for k in range(2):
                    last = mm(ps[0:COLS, 0, 0:COLS], cwt_48[:, k, :], cwt_48[:, k, :], k == 0, k == 1)
                last.then_inc(setup_pe, 1)
                pe.wait_ge(setup_dve, DVE_GRAM)
                for t in range(TILES):
                    pair = t // (TILES // 2)
                    last = mm(ps[:, 1, IMAGE_PAIR * t:IMAGE_PAIR * (t + 1)], paired_sb[:, 128 * t:128 * (t + 1)],
                              gram_48[:, IMAGE_PAIR * pair:IMAGE_PAIR * (pair + 1)])
                last.then_inc(setup_pe, 1)
                pe.wait_ge(wqkv_landed, 32)
                for j in range(4):
                    o = ps[0:E2, 3, 128 * j:128 * (j + 1)]
                    for k in range(2):
                        mm(o, wqkv_sb[:, k, E2 * j:E2 * (j + 1)], cwt[:, k, :], k == 0, False)
                    last = mm(o, bqkv_sb[0:1, E2 * j:E2 * (j + 1)], cr[0:1, ROW_ONE_P:ROW_ONE_P + 128], False, True)
                last.then_inc(setup_pe, 1)
                pe.wait_ge(setup_act, ACT_QKT)
                for j in range(2):
                    last = mm(ps[:, 1, 0:128], qkt[:, 2 + j, :], qkt[:, j, :], j == 0, j == 1)
                last.then_inc(setup_pe, 1)
                pe.wait_ge(setup_dve, DVE_MIX)
                for k in range(2):
                    for j in range(2):
                        last = mm(ps[0:E2, 2 + k if j == 0 else 6 + k, 0:384], mix_in[:, E2 * k:E2 * (k + 1)],
                                  cr[0:MIXES, ROW_OUT + 384 * j:ROW_OUT + 384 * (j + 1)])
                last.then_inc(setup_pe, 1)
                for j in range(2):
                    mm(ps[0:1, 4 + j, 0:384], mix[:], cr[0:MIXES, ROW_OUT + 384 * j:ROW_OUT + 384 * (j + 1)])
                pe.wait_ge(setup_act, ACT_COEF)
                mm(ps[0:1, 6, 0:EMBED], mix[:], cr[0:MIXES, ROW_IN:ROW_IN + EMBED])
                pe.wait_ge(wfc_landed, 32)
                for k in range(2):
                    for t in range(4):
                        pe.transpose(ps[0:E2, 2 + k, 128 * t:128 * (t + 1)], wfc_sb[:, t, E2 * k:E2 * (k + 1)], ident)
                for k in range(2):
                    for t in range(4, HT):
                        last = pe.transpose(ps[0:E2, 7, 256 * k + 128 * (t - 4):256 * k + 128 * (t - 3)],
                                            wfc_sb[:, t, E2 * k:E2 * (k + 1)], ident)
                last.then_inc(setup_pe, 1)

            def setup_basis():
                pe.wait_ge(setup_act, ACT_W0T)
                pe.wait_ge(setup_dve, DVE_BIAS)
                for at in (0, 256):
                    o = ps[:, 3, at:at + EMBED]
                    mm(o, cr[:, ROW_P:ROW_P + 128], cw_sb[:], True, False)
                    for k in range(2):
                        mm(o, cwt_ctx[:, k, :], wqkv_sb[:, k, 2 * EMBED:3 * EMBED], False, False)
                    last = mm(o, cr[0:1, ROW_ONE_U:ROW_ONE_U + 128], bqkv_sb[0:1, 2 * EMBED:3 * EMBED], False, at == 0)
                    if at:
                        last = mm(o, cr[0:1, ROW_ONE_U:ROW_ONE_U + 128], bproj_sb[0:1, :], False, True)
                last.then_inc(setup_pe, 1)

            def setup_gram():
                pe.wait_ge(setup_dve, DVE_CENTRED)
                for k in range(2):
                    last = pe.transpose(ps[0:E2, 2, 128 * k:128 * (k + 1)], basis_c[:, E2 * k:E2 * (k + 1)], ident)
                last.then_inc(setup_pe, 1)
                pe.wait_ge(setup_act, ACT_BT)
                for k in range(2):
                    last = mm(ps[:, 1, 0:128], basis_t[:, k, :], basis_t[:, k, :], k == 0, k == 1)
                last.then_inc(setup_pe, 1)

            def setup_f():
                pe.wait_ge(setup_pool, POOL_W0T)
                for j in range(2):
                    o = ps[:, 4 + j, 0:384]
                    for k in range(2):
                        mm(o, basis_t[:, k, :], w0t[:, k, 384 * j:384 * (j + 1)], k == 0, False)
                    last = mm(o, cr[0:1, ROW_ONE_F:ROW_ONE_F + 128], bfc_sb[0:1, 384 * j:384 * (j + 1)], False, True)
                last.then_inc(setup_pe, 1)

            def setup_w1():
                pe.wait_ge(setup_pool, POOL_WPROJ)
                pe.wait_ge(setup_dve, DVE_F)
                for t in range(HT):
                    for k in range(2):
                        at = EMBED * (t % 2) + E2 * k
                        last = pe.transpose(ps[:, (4, 6, 7)[t // 2], at:at + E2], wproj_sb[:, k, 128 * t:128 * (t + 1)],
                                            ident[0:E2, 0:E2])
                last.then_inc(setup_pe, 1)

            def sum_rows(n, pair):
                first_tile = TILES // 2 * pair
                for t in range(first_tile, first_tile + TILES // 2):
                    pe.wait_ge(reduced, SLOTS * n + 2 * t + 2)
                for h in range(2):
                    o = ps[0:HALF, 0, 2 * COLS * h:2 * COLS * (h + 1)].rearrange("p (g c) -> p g c", g=2)[
                        :, :, IMAGE_PAIR * pair:IMAGE_PAIR * (pair + 1)]
                    for t in range(first_tile, first_tile + TILES // 2):
                        last = mm(o, pooled[:, t, HALF * h:HALF * (h + 1)], sel_gram[:, t], t == first_tile,
                                  t == first_tile + TILES // 2 - 1)
                last.then_inc(pool_summed, 1)

            def turn_phat(m):
                pe.wait_ge(phat_tok_ready, 2 * m + 2)
                for h in range(2):
                    last = pe.transpose(ps[:, 0, HALF * h:HALF * (h + 1)],
                                        phat_tok[:, h].rearrange("p b r -> p (b r)"), ident[0:HALF, 0:HALF])
                last.then_inc(phat_turned, 1)

            def apply_a(m):
                pe.wait_ge(phat_rows_ready, m + 1)
                mm(ps[:, 0, 0:TOKENS], score_mat[:], phat_rows[:]).then_inc(b_summed, 1)

            def scores(m):
                pe.wait_ge(b_rows_ready, m + 1)
                if first(m):
                    pe.wait_ge(setup_dve, DVE_G2)
                for h in range(2):
                    for b in range(GROUP):
                        last = mm(ps[0:HALF, b, TOKENS * h:TOKENS * (h + 1)],
                                  phat_rows[Q * b:Q * (b + 1), HALF * h:HALF * (h + 1)], b_rows[Q * b:Q * (b + 1), :])
                        if h == 1:
                            last.then_inc(scores_ready, 1)

            def turn_probs(m):
                for b in range(GROUP):
                    pe.wait_ge(probs_ready, 4 * m + b + 1)
                    for k in range(2):
                        for h in range(2):
                            at = TOKENS * k + HALF * h
                            last = pe.transpose(ps[0:HALF, b, at:at + HALF],
                                                probs[:, b, h, HALF * k:HALF * (k + 1)], ident[0:HALF, 0:HALF])
                    last.then_inc(probs_turned, 1)

            def weigh(m):
                pe.wait_ge(probs_t_ready, 4 * m + 4)
                for k in range(2):
                    for b in range(GROUP):
                        last = mm(ps[Q * b:Q * (b + 1), 1, 0:TOKENS], phat_tok[:, k, b, :], probs_t[:, b, k, :],
                                  k == 0, k == 1)
                last.then_inc(context_summed, 1)

            def turn_context(m):
                pe.wait_ge(context_rows_ready, m + 1)
                for h in range(2):
                    last = pe.transpose(ps[0:HALF, 1, 256 + 128 * h:256 + 128 * (h + 1)],
                                        context_rows[:, HALF * h:HALF * (h + 1)], ident)
                last.then_inc(context_ready, 1)

            def turn_u(m):
                pe.wait_ge(u_tok_ready, m + 1)
                pe.wait_ge(p_in_u_ready, m + 1)
                for h in range(2):
                    last = pe.transpose(ps[:, 2, HALF * h:HALF * (h + 1)],
                                        u_tok[:, h].rearrange("p b r -> p (b r)"), ident[0:HALF, 0:HALF])
                last.then_inc(u_turned, 1)

            def apply_g2(m):
                pe.wait_ge(u_rows_ready, m + 1)
                for h in range(2):
                    last = mm(ps[0:HALF, 1, 128 * h:128 * (h + 1)], u_rows[:, HALF * h:HALF * (h + 1)], g2[:])
                last.then_inc(g2_summed, 1)

            def turn_uhat(m):
                pe.wait_ge(uhat_tok_ready, 2 * m + 2)
                if first(m):
                    pe.wait_ge(setup_act, ACT_W1)
                else:
                    pe.wait_ge(gelu_done, 12 * m)
                for b in range(GROUP):
                    for h in range(2):
                        at = TOKENS * (b % 2) + HALF * h
                        last = pe.transpose(ps[:, HB + b // 2, at:at + HALF],
                                            uhat_tok[:, h, b].rearrange("p c r -> p (c r)"),
                                            ident[0:HALF, 0:HALF])
                last.then_inc(uhat_turned, 1)

            def hidden(f, unit):
                if unit == 0:
                    pe.wait_ge(uhat_ready, f + 1)
                if not (first(f) and unit < 2):
                    pe.wait_ge(gelu_done, 12 * f + unit - 1)
                half, t = divmod(unit, HT)
                mm(ps[:, HB + unit % 2, 0:PAIR_TOKENS], f_stack[:, 128 * t:128 * (t + 1)],
                   uhat_stack[:, PAIR_TOKENS * half:PAIR_TOKENS * (half + 1)]).then_inc(hidden_summed, 1)

            def project(f, part):
                half = part // 12
                if first(f) and part == 0:
                    pe.wait_ge(setup_pool, POOL_W1)
                for r in range(2 * (part % 12), 2 * (part % 12) + 2):
                    tile, t = divmod(r, HT)
                    b, h = 2 * half + tile // 2, tile % 2
                    o = ps[0:HALF, OB + tile % 2, 0:EMBED]
                    if t == 0:
                        if not (first(f) and half == 0 and tile < 2):
                            pe.wait_ge(out_ready, 8 * f + 4 * half + tile - 1)
                        pe.wait_ge(u_kept_ready[half], f + 1)
                        mm(o, u_kept[half][:, HALF * h:HALF * (h + 1)], resid[:, b], True, False)
                    if tile == 0:
                        pe.wait_ge(h_lo_ready, 12 * f + HT * half + t + 1)
                    at = slice(HALF * tile, HALF * (tile + 1))
                    mm(o, h_hi[:, half, t, at], w1_hi[:, t, :], False, False)
                    mm(o, h_hi[:, half, t, at], w1_lo[:, t, :], False, False)
                    last = mm(o, h_lo[:, half, t, at], w1_hi[:, t, :], False, t == HT - 1)
                    if t == HT - 1:
                        last.then_inc(out_summed, 1)

            SETUP = {"basis": setup_basis, "gram": setup_gram, "f": setup_f, "w1": setup_w1}

            def iteration(n, on):
                for step in range(STEPS):
                    for k in sorted(on, reverse=True):
                        m, now = n - k, STEPS * k + step
                        at = order(PE_ORDER, m)
                        if now == at["sum_rows"][0]:
                            sum_rows(m, 0)
                        if now == at["sum_rows"][1]:
                            sum_rows(m, 1)
                        if now == at["turn_phat"]:
                            turn_phat(m)
                        if now == at["apply_a"]:
                            apply_a(m)
                        if now == at["scores"]:
                            scores(m)
                        if now == at["turn_probs"]:
                            turn_probs(m)
                        if now == at["weigh"]:
                            weigh(m)
                        if now == at["turn_context"]:
                            turn_context(m)
                        if now == at["turn_u"]:
                            turn_u(m)
                        if now == at["apply_g2"]:
                            apply_g2(m)
                        if now == at["turn_uhat"]:
                            turn_uhat(m)
                        for unit in range(2 * HT):
                            if now == at["hidden"][unit]:
                                hidden(m, unit)
                        for part in range(24):
                            if now == at["project"][part]:
                                project(m, part)
                    for piece, build_piece in SETUP.items():
                        if is_step(n, PE_SETUP[piece][0]) and step == PE_SETUP[piece][1]:
                            build_piece()

            setup()
            run(pe, iteration)

        @block.scalar
        def _(act):
            def setup():
                act.wait_ge(setup_pe, PE_CWT)
                act.copy(cwt_48[:], ps[0:E2, 2, 0:2 * COLS].rearrange("p (k c) -> p k c", k=2))
                act.copy(cwt, ps[0:E2, 0, 0:256].rearrange("p (k c) -> p k c", k=2))
                act.copy(cwt_ctx[:], ps[0:E2, 0, 256:512].rearrange("p (k c) -> p k c", k=2)).then_inc(setup_act, 1)
                act.wait_ge(setup_pe, PE_ROWS)
                act.copy(sel_gram[:, :, 1, :],
                         ps[:, 1, 0:TILES * IMAGE_PAIR].rearrange("p (t c) -> p t c", t=TILES)).then_inc(setup_act, 1)
                act.wait_ge(setup_pe, PE_QKT)
                act.copy(qkt[:], ps[0:E2, 3, :].rearrange("p (j c) -> p j c", j=4)).then_inc(setup_act, 1)
                act.wait_ge(setup_pe, PE_COEF)
                act.copy(coef[:, :, 0:384], ps[0:E2, 2:4, 0:384])
                act.copy(coef[:, :, 384:768], ps[0:E2, 6:8, 0:384]).then_inc(setup_act, 1)
                act.wait_ge(setup_pe, PE_W0T)
                act.copy(w0t[:, :, 0:512], ps[0:E2, 2:4, :])
                act.copy(w0t[:, :, 512:768],
                         ps[0:E2, 7, :].rearrange("p (k c) -> p k c", k=2)).then_inc(setup_act, 1)

            def setup_basis():
                act.wait_ge(setup_pe, PE_BT)
                act.copy(basis_t[:], ps[0:E2, 2, 0:256].rearrange("p (k c) -> p k c", k=2)).then_inc(setup_act, 1)

            def setup_f():
                act.wait_ge(setup_pe, PE_F)
                act.copy(f_hi.rearrange("p (k c) -> p k c", k=2), ps[:, 4:6, 0:384]).then_inc(setup_act, 1)

            def setup_w1():
                act.wait_ge(setup_pe, PE_W1)
                act.copy(w1_f32[:, 0:2, :], ps[:, 4, 0:384].rearrange("p (t e) -> p t e", t=2))
                act.copy(w1_f32[:, 2:6, :].rearrange("p (a t) e -> p a (t e)", a=2), ps[:, 6:8, 0:384])
                act.copy(w1_hi[:, 0:2, :], ps[:, 4, 0:384].rearrange("p (t e) -> p t e", t=2))
                act.copy(w1_hi[:, 2:6, :].rearrange("p (a t) e -> p a (t e)", a=2),
                         ps[:, 6:8, 0:384]).then_inc(setup_act, 1)

            def copy_p_tok(m):
                act.wait_ge(pool_summed, 2 * m + 2)
                if not first(m):
                    act.wait_ge(p_in_u_ready, m)
                sums = ps[0:HALF, 0, 0:4 * COLS].rearrange("p (h g c) -> p h g c", h=2, g=2)
                act.copy(p_tok[:].rearrange("p h b r -> p h (b r)"), sums[:, :, 0, :]).then_inc(p_tok_ready, 1)

            def copy_phat(m):
                act.wait_ge(phat_turned, m + 1)
                act.copy(phat_rows[:], ps[:, 0, 0:TOKENS]).then_inc(phat_rows_ready, 1)

            def copy_b(m):
                act.wait_ge(b_summed, m + 1)
                act.copy(b_rows[:], ps[:, 0, 0:TOKENS]).then_inc(b_rows_ready, 1)

            def exponentials(m):
                for b in range(GROUP):
                    act.wait_ge(max_ready, 4 * m + b + 1)
                    for h in range(2):
                        last = act.activation(probs[:, b, h, :], ps[0:HALF, b, TOKENS * h:TOKENS * (h + 1)], ACT.Exp,
                                              bias=neg_max[:, b, h:h + 1])
                    last.then_inc(probs_ready, 1)

            def copy_probs(m):
                for b in range(GROUP):
                    act.wait_ge(probs_turned, 4 * m + b + 1)
                    act.copy(probs_t[:, b].rearrange("p k q -> p (k q)"),
                             ps[0:HALF, b, 0:PAIR_TOKENS]).then_inc(probs_t_ready, 1)

            def copy_context(m):
                act.wait_ge(context_summed, m + 1)
                act.copy(context_rows[:], ps[:, 1, 0:TOKENS]).then_inc(context_rows_ready, 1)

            def copy_u(m):
                act.wait_ge(u_turned, m + 1)
                if not first(m):
                    act.wait_ge(u_kept_ready[0], m)
                act.copy(u_rows[:], ps[:, 2, 0:TOKENS]).then_inc(u_rows_ready, 1)

            def copy_uhat(m):
                act.wait_ge(uhat_turned, m + 1)
                act.copy(uhat_hi[:].rearrange("p (k c) -> p k c", k=2),
                         ps[:, HB:HB + 2, 0:PAIR_TOKENS]).then_inc(uhat_hi_ready, 1)

            def gelu(f, unit):
                half, t = divmod(unit, HT)
                if not (first(f) and unit < 4):
                    act.wait_ge(h_lo_ready, 12 * f + unit - 3)
                if t == 0 and not first(f):
                    act.wait_ge(out_summed, 8 * f - 4 + 4 * half)
                act.wait_ge(hidden_summed, 12 * f + unit + 1)
                summed = ps[:, HB + unit % 2, 0:PAIR_TOKENS]
                act.activation(h_f32[:, unit % 4, :], summed, ACT.Gelu_apprx_tanh)
                act.activation(h_hi[:, half, t, :], summed, ACT.Gelu_apprx_tanh).then_inc(gelu_done, 1)

            def take_out(f, unit):
                half, tile = divmod(unit, 4)
                act.wait_ge(out_summed, 8 * f + 4 * half + tile + 1)
                if tile == 0 and not first(f):
                    act.wait_ge(out_sent[half], 16 * f)
                act.copy(out_sb[0:HALF, half, tile, :], ps[0:HALF, OB + tile % 2, 0:EMBED]).then_inc(out_ready, 1)

            SETUP = {"basis": setup_basis, "f": setup_f, "w1": setup_w1}

            def iteration(n, on):
                for step in range(STEPS):
                    for k in sorted(on, reverse=True):
                        m, now = n - k, STEPS * k + step
                        at = order(ACT_ORDER, m)
                        if now == at["copy_p_tok"]:
                            copy_p_tok(m)
                        if now == at["copy_phat"]:
                            copy_phat(m)
                        if now == at["copy_b"]:
                            copy_b(m)
                        if now == at["exponentials"]:
                            exponentials(m)
                        if now == at["copy_probs"]:
                            copy_probs(m)
                        if now == at["copy_context"]:
                            copy_context(m)
                        if now == at["copy_u"]:
                            copy_u(m)
                        if now == at["copy_uhat"]:
                            copy_uhat(m)
                        for unit in range(2 * HT):
                            if now == at["gelu"][unit]:
                                gelu(m, unit)
                        for tile in range(8):
                            if now == at["take_out"][tile]:
                                take_out(m, tile)
                    for piece, build_piece in SETUP.items():
                        if is_step(n, ACT_SETUP[piece][0]) and step == ACT_SETUP[piece][1]:
                            build_piece()

            setup()
            run(act, iteration)

        @block.gpsimd
        def _(pool):
            def setup():
                pool.memset(stat[:], 1.0).then_inc(setup_pool_self, 1)
                pool.memset(phat_tok[:], 0.0).then_inc(setup_pool_self, 1)
                pool.memset(u_tok[:], 0.0).then_inc(setup_pool_self, 1)
                pool.memset(uhat_tok[:], 0.0).then_inc(setup_pool_self, 1)
                pool.wait_ge(setup_pool_self, 4)
                pool.memset(phat_tok[:, :, :, ONE_P:ONE_P + 1], 1.0).then_inc(setup_pool_self, 1)
                pool.memset(u_tok[:, :, :, ONE_U:ONE_U + 1], 1.0).then_inc(setup_pool_self, 1)
                pool.memset(uhat_tok[:, :, :, :, ONE_F:ONE_F + 1].rearrange("p h b c r -> p (h b) c r"),
                            1.0).then_inc(setup_pool_self, 1)
                pool.memset(zero[:], 0.0).then_inc(setup_pool_self, 1)
                pool.memset(three_halves[:], 1.5).then_inc(setup_pool_self, 1)
                pool.wait_ge(setup_pool_self, 9)
                pool.wait_ge(setup_act, ACT_W0T)
                pool.tensor_tensor(w0t, w0t, coef, ALU.mult).then_inc(setup_pool, 1)
                pool.wait_ge(wproj_landed, 32)
                pool.tensor_tensor(wproj_sb[:], wproj_sb[:], coef, ALU.mult).then_inc(setup_pool, 1)

            def setup_w1():
                pool.wait_ge(setup_act, ACT_W1)
                pool.tensor_tensor(w1_lo[:], w1_f32, w1_hi[:].bitcast(F32), ALU.subtract).then_inc(setup_pool, 1)

            inv_std = stat[:, 2].rearrange("p k (h b) -> p k h b", h=2)

            def inverse_roots(n):
                at = 12 * (n - 1)
                pool.wait_ge(stat_steps, 4 * n)
                h, y = stat[:, 3], stat[:, 2]
                for step in range(3):
                    pool.tensor_tensor(newton[:], y, y, ALU.mult).then_inc(newton_steps, 1)
                    pool.wait_ge(newton_steps, at + 4 * step + 1)
                    pool.tensor_tensor(newton[:], newton[:], h, ALU.mult).then_inc(newton_steps, 1)
                    pool.wait_ge(newton_steps, at + 4 * step + 2)
                    pool.tensor_tensor(newton[:], newton[:], three_halves[:], ALU.add).then_inc(newton_steps, 1)
                    pool.wait_ge(newton_steps, at + 4 * step + 3)
                    pool.tensor_tensor(y, y, newton[:], ALU.mult).then_inc(newton_steps, 1)
                    pool.wait_ge(newton_steps, at + 4 * step + 4)

            def scale_p(m):
                if not first(m):
                    pool.wait_ge(context_summed, m)
                for h in range(2):
                    pool.tensor_tensor(phat_tok[:, h, :, 0:CHANNELS], p_tok[:, h],
                                       inv_std[:, 0, h, :].unsqueeze(2).broadcast_to([HALF, GROUP, CHANNELS]),
                                       ALU.mult).then_inc(phat_tok_ready, 1)

            def scale_u():
                shape = [HALF, GROUP, 4, BASIS]
                for h in range(2):
                    pool.tensor_tensor(uhat_tok[:, h, :, :, 0:BASIS],
                                       u_tok[:, h, :, 0:BASIS].unsqueeze(2).broadcast_to(shape),
                                       inv_std[:, 1, h, :].unsqueeze(2).unsqueeze(3).broadcast_to(shape),
                                       ALU.mult).then_inc(uhat_tok_ready, 1)

            def low_part(f, unit):
                half, t = divmod(unit, HT)
                pool.wait_ge(gelu_done, 12 * f + unit + 1)
                pool.tensor_tensor(h_lo[:, half, t, :], h_f32[:, unit % 4, :], h_hi[:, half, t, :].bitcast(F32),
                                   ALU.subtract).then_inc(h_lo_ready, 1)

            def p_columns(a):
                return a[:, :, :, 0:CHANNELS].rearrange("p h b r -> p (h b) r")

            zeros = zero[0:HALF, :].unsqueeze(2).broadcast_to([HALF, 2 * GROUP, CHANNELS])

            def p_into_u(m):
                if not first(m):
                    pool.wait_ge(uhat_tok_ready, 2 * m)
                pool.tensor_tensor(p_columns(u_tok), p_tok[:].rearrange("p h b r -> p (h b) r"), zeros,
                                   ALU.add).then_inc(p_in_u_ready, 1)

            def keep_u(f, half):
                if half == 0:
                    pool.wait_ge(u_rows_ready, f + 1)
                else:
                    pool.wait_ge(u_kept_ready[0], f + 1)
                if not first(f):
                    pool.wait_ge(out_summed, 8 * f - 4 + 4 * half)
                    if half == 0:
                        pool.wait_ge(u_kept_ready[1], f)
                pool.tensor_tensor(u_kept[half][:], (u_rows, u_kept[0])[half][:],
                                   zero[:].broadcast_to([128, TOKENS]), ALU.add).then_inc(u_kept_ready[half], 1)

            def iteration(n, on):
                for step in range(STEPS):
                    if is_step(n, 2) and step == 0:
                        setup_w1()
                    if step == 0 and (1 in on or 2 in on):
                        inverse_roots(n)
                        if 1 in on:
                            scale_p(n - 1)
                        if 2 in on:
                            scale_u()
                    for k in sorted(on, reverse=True):
                        m, now = n - k, STEPS * k + step
                        at = order(POOL_ORDER, m)
                        if now == at["p_into_u"]:
                            p_into_u(m)
                        if now == at["keep_u"][0]:
                            keep_u(m, 0)
                        if now == at["keep_u"][1]:
                            keep_u(m, 1)
                        for unit in range(2 * HT):
                            if now == at["low_part"][unit]:
                                low_part(m, unit)

            setup()
            run(pool, iteration)


def kernel(x, L0_tok_channel_weights, L0_attn_W_qkv, L0_attn_b_qkv, L0_ffn_w_fc, L0_ffn_b_fc, L0_ffn_w_proj,
           L0_ffn_b_proj, L0_ffn_alpha_e, L0_ffn_alpha_r):
    import concourse.bacc as bacc
    from concourse.bass_utils import run_bass_kernel_spmd

    full, rows, paired = constants()
    arrays = {
        "x": x, "cw": L0_tok_channel_weights, "wqkv": L0_attn_W_qkv, "bqkv": L0_attn_b_qkv.reshape(1, -1),
        "wfc": L0_ffn_w_fc, "bfc": L0_ffn_b_fc.reshape(1, -1), "wproj": L0_ffn_w_proj,
        "bproj": L0_ffn_b_proj.reshape(1, -1),
        "alpha_e": np.repeat(L0_ffn_alpha_e, len(RATIO_CHOICES)).reshape(-1, 1),
        "alpha_r": np.tile(L0_ffn_alpha_r, len(EMBED_CHOICES)).reshape(-1, 1),
        "const_full": full, "const_rows": rows, "const_paired": paired,
    }
    arrays = {k: np.ascontiguousarray(v) for k, v in arrays.items()}
    nc = bacc.Bacc("TRN2", target_bir_lowering=False, num_devices=1)
    args = [nc.dram_tensor(k, v.shape, F32, kind="ExternalInput").ap() for k, v in arrays.items()]
    out = nc.dram_tensor("out", (IMAGES, TOKENS, EMBED), F32, kind="ExternalOutput").ap()
    build(nc, *args, out)
    r = run_bass_kernel_spmd(nc, [arrays], core_ids=[0])
    return r.results[0]["out"]
```
